# Optimizing a Trainium2 kernel written in Bass

```python
import numpy as np
import jax
import jax.numpy as jnp

def _softmax(x, axis=-1):
    return jax.nn.softmax(x, axis=axis)

def _gelu(x):
    return jax.nn.gelu(x, approximate=True)

def _silu(x):
    return jax.nn.silu(x)

def _sigmoid(x):
    return jax.nn.sigmoid(x)

def _layernorm(x, axis=-1, eps=1e-05):
    m = jnp.mean(x, axis=axis, keepdims=True)
    v = jnp.var(x, axis=axis, keepdims=True)
    return (x - m) / jnp.sqrt(v + eps)

def _scatter_add(tgt, idx, src, axis=0):
    return tgt.at[idx].add(src)

def _segment_sum(src, seg, n):
    return jax.ops.segment_sum(src, seg, n)
kernel_name = 'mk_cond_resid_d4_seqx_r2_8cd747'

def setup_inputs(seed: int=0):
    np.random.seed(seed)
    _w = jnp.asarray

    def _rec_inputs():
        import jax
        import jax.numpy as jnp
        _rk = jax.random.key(seed)
        x = -0.000125 + 0.9999 * jax.random.normal(jax.random.fold_in(_rk, 1), (8, 512, 512), jnp.float32)
        _lenS = 512 - jax.random.randint(jax.random.fold_in(_rk, 7), (8,), 0, max(1, 512 // 4) + 1, jnp.int32)
        _lenS2 = 512 - jax.random.randint(jax.random.fold_in(_rk, 8), (8,), 0, max(1, 512 // 4) + 1, jnp.int32)
        cond_1024 = -0.00493535 + 1.00056 * jax.random.normal(jax.random.fold_in(_rk, 11), (8, 512), jnp.float32)
        _validS = jnp.arange(512)[None, :] < _lenS[:, None]
        _validS2 = jnp.arange(512)[None, :] < _lenS2[:, None]
        _causal = jnp.tril(jnp.ones((512, 512), dtype=bool))
        mask_Bx1x1xS_ff0 = jnp.where(jnp.ones((8, 1, 1, 512), dtype=bool), 0.0, -1000000000.0).astype(jnp.float32)
        return (x, cond_1024, mask_Bx1x1xS_ff0)
    x, cond_1024, mask_Bx1x1xS_ff0 = _rec_inputs()

    def _L0_cond_setup():
        import jax, jax.numpy as jnp
        import numpy as np
        INPUT_DIM = 512
        LATENT_DIM = 512
        key = jax.random.key(seed)
        ks = jax.random.split(key, 8)
        B, T = (64, 256)
        concat_dim = INPUT_DIM + LATENT_DIM
        s = lambda fan_in: 1.0 / np.sqrt(fan_in)
        return {'x': jax.random.normal(ks[0], (B, T, INPUT_DIM), dtype=jnp.float32), 'h0': jax.random.normal(ks[1], (B, LATENT_DIM), dtype=jnp.float32), 'w_W': jax.random.uniform(ks[2], (concat_dim, 2 * LATENT_DIM), jnp.float32, -s(concat_dim), s(concat_dim)), 'w_b': jax.random.uniform(ks[3], (2 * LATENT_DIM,), jnp.float32, -s(concat_dim), s(concat_dim)), 'wx_W': jax.random.uniform(ks[4], (INPUT_DIM, LATENT_DIM), jnp.float32, -s(INPUT_DIM), s(INPUT_DIM)), 'wx_b': jax.random.uniform(ks[5], (LATENT_DIM,), jnp.float32, -s(INPUT_DIM), s(INPUT_DIM)), 'wh_W': jax.random.uniform(ks[6], (LATENT_DIM, LATENT_DIM), jnp.float32, -s(LATENT_DIM), s(LATENT_DIM)), 'wh_b': jax.random.uniform(ks[7], (LATENT_DIM,), jnp.float32, -s(LATENT_DIM), s(LATENT_DIM))}
    _L0_cond_all = _L0_cond_setup()
    _L0_cond_in = {k: v for k, v in _L0_cond_all.items() if k in ('w_W', 'w_b', 'wx_W', 'wx_b', 'wh_W', 'wh_b')}
    del _L0_cond_all

    def _L1_cond_setup():
        import jax, jax.numpy as jnp
        import numpy as np
        import math
        N, T, D, H = (128, 256, 512, 512)
        key = jax.random.key(seed)
        k1, k2, k3, k4 = jax.random.split(key, 4)
        x = jax.random.normal(k1, (N, T, D), dtype=jnp.float32)
        h0 = jax.random.normal(k2, (N, H), dtype=jnp.float32)
        Wx = jax.random.normal(k3, (D, H), dtype=jnp.float32) / math.sqrt(D)
        Wh = jax.random.normal(k4, (H, H), dtype=jnp.float32) / math.sqrt(H)
        b = jnp.zeros((H,), dtype=jnp.float32)
        return {'x': x, 'h0': h0, 'Wx': Wx, 'Wh': Wh, 'b': b}
    _L1_cond_all = _L1_cond_setup()
    _L1_cond_in = {k: v for k, v in _L1_cond_all.items() if k in ('Wx', 'Wh', 'b')}
    del _L1_cond_all

    def _L2_cond_setup():
        import jax, jax.numpy as jnp
        import numpy as np
        N, T, D, H = (64, 256, 512, 512)
        key = jax.random.key(seed)
        k1, k2, k3, k4 = jax.random.split(key, 4)
        x = jax.random.normal(k1, (N, T, D), dtype=jnp.float32)
        h0 = jax.random.normal(k2, (N, H), dtype=jnp.float32)
        Wx = jax.random.normal(k3, (D, H), dtype=jnp.float32) / jnp.sqrt(jnp.float32(D))
        Wh = jax.random.normal(k4, (H, H), dtype=jnp.float32) / jnp.sqrt(jnp.float32(H))
        b = jnp.zeros((H,), dtype=jnp.float32)
        return {'x': x, 'h0': h0, 'Wx': Wx, 'Wh': Wh, 'b': b}
    _L2_cond_all = _L2_cond_setup()
    _L2_cond_in = {k: v for k, v in _L2_cond_all.items() if k in ('Wx', 'Wh', 'b')}
    del _L2_cond_all

    def _L3_cond_setup():
        import jax, jax.numpy as jnp
        import numpy as np
        EMBED = 512
        HEADS = 16
        HDIM = EMBED // HEADS
        MASK_OUT = -10000.0

        def _split_heads(t):
            B, T, _ = t.shape
            return t.reshape(B, T, HEADS, HDIM).transpose(0, 2, 1, 3)
        key = jax.random.key(seed)
        ks = jax.random.split(key, 12)
        B, S = (4, 1023)
        scale = 0.02
        return {'word_hidden_states': jax.random.normal(ks[0], (B, S, EMBED), jnp.float32), 'image_hidden_states': jax.random.normal(ks[1], (B, EMBED), jnp.float32), 'attention_mask': jnp.zeros((B, 1, 1, S), jnp.float32), 'c_attn_w': jax.random.normal(ks[2], (EMBED, 3 * EMBED), jnp.float32) * scale, 'c_attn_b': jnp.zeros((3 * EMBED,), jnp.float32), 'c_proj_w': jax.random.normal(ks[3], (EMBED, EMBED), jnp.float32) * scale, 'c_proj_b': jnp.zeros((EMBED,), jnp.float32), 'uk_w': jax.random.normal(ks[4], (EMBED, EMBED), jnp.float32) * scale, 'uk_b': jnp.zeros((EMBED,), jnp.float32), 'uv_w': jax.random.normal(ks[5], (EMBED, EMBED), jnp.float32) * scale, 'uv_b': jnp.zeros((EMBED,), jnp.float32)}
    _L3_cond_all = _L3_cond_setup()
    _L3_cond_in = {k: v for k, v in _L3_cond_all.items() if k in ('c_attn_w', 'c_attn_b', 'c_proj_w', 'c_proj_b', 'uk_w', 'uk_b', 'uv_w', 'uv_b')}
    del _L3_cond_all
    return {'x': x, 'cond_1024': cond_1024, 'mask_Bx1x1xS_ff0': mask_Bx1x1xS_ff0, 'L0_cond_w_W': _L0_cond_in['w_W'], 'L0_cond_w_b': _L0_cond_in['w_b'], 'L0_cond_wx_W': _L0_cond_in['wx_W'], 'L0_cond_wx_b': _L0_cond_in['wx_b'], 'L0_cond_wh_W': _L0_cond_in['wh_W'], 'L0_cond_wh_b': _L0_cond_in['wh_b'], 'L1_cond_Wx': _L1_cond_in['Wx'], 'L1_cond_Wh': _L1_cond_in['Wh'], 'L1_cond_b': _L1_cond_in['b'], 'L2_cond_Wx': _L2_cond_in['Wx'], 'L2_cond_Wh': _L2_cond_in['Wh'], 'L2_cond_b': _L2_cond_in['b'], 'L3_cond_c_attn_w': _L3_cond_in['c_attn_w'], 'L3_cond_c_attn_b': _L3_cond_in['c_attn_b'], 'L3_cond_c_proj_w': _L3_cond_in['c_proj_w'], 'L3_cond_c_proj_b': _L3_cond_in['c_proj_b'], 'L3_cond_uk_w': _L3_cond_in['uk_w'], 'L3_cond_uk_b': _L3_cond_in['uk_b'], 'L3_cond_uv_w': _L3_cond_in['uv_w'], 'L3_cond_uv_b': _L3_cond_in['uv_b']}

def reference(x, cond_1024, mask_Bx1x1xS_ff0, L0_cond_w_W, L0_cond_w_b, L0_cond_wx_W, L0_cond_wx_b, L0_cond_wh_W, L0_cond_wh_b, L1_cond_Wx, L1_cond_Wh, L1_cond_b, L2_cond_Wx, L2_cond_Wh, L2_cond_b, L3_cond_c_attn_w, L3_cond_c_attn_b, L3_cond_c_proj_w, L3_cond_c_proj_b, L3_cond_uk_w, L3_cond_uk_b, L3_cond_uv_w, L3_cond_uv_b):
    import jax
    import jax.numpy as jnp

    def _L0_cond_ref(x, h0, w_W, w_b, wx_W, wx_b, wh_W, wh_b):
        import jax, jax.numpy as jnp
        import numpy as np
        INPUT_DIM = 512
        LATENT_DIM = 512
        xT = jnp.swapaxes(x, 0, 1)

        def step(h, x_t):
            fused = jax.nn.sigmoid(jnp.concatenate([x_t, h], axis=-1) @ w_W + w_b)
            hidden_state, output_state = jnp.split(fused, 2, axis=-1)
            memory_state = x_t @ wx_W + wx_b + hidden_state * (h @ wh_W + wh_b)
            h_new = output_state * h + (1.0 - output_state) * jnp.tanh(memory_state)
            return (h_new, h_new)
        _, hs = jax.lax.scan(step, h0, xT)
        return jnp.swapaxes(hs, 0, 1)

    def _L1_cond_ref(x, h0, Wx, Wh, b):
        import jax, jax.numpy as jnp
        import numpy as np
        import math
        N, T, D, H = (128, 256, 512, 512)
        xw = jnp.einsum('ntd,dh->nth', x, Wx) + b

        def step(h_prev, xw_t):
            h_next = jnp.tanh(xw_t + h_prev @ Wh)
            return (h_next, h_next)
        _, hs = jax.lax.scan(step, h0, jnp.swapaxes(xw, 0, 1))
        return jnp.swapaxes(hs, 0, 1)

    def _L2_cond_ref(x, h0, Wx, Wh, b):
        import jax, jax.numpy as jnp
        import numpy as np
        N, T, D, H = (64, 256, 512, 512)
        xw = jnp.einsum('ntd,dh->nth', x, Wx) + b

        def step(prev_h, xw_t):
            next_h = jnp.tanh(xw_t + prev_h @ Wh)
            return (next_h, next_h)
        _, hs = jax.lax.scan(step, h0, jnp.swapaxes(xw, 0, 1))
        return jnp.swapaxes(hs, 0, 1)

    def _L3_cond_ref(word_hidden_states, image_hidden_states, attention_mask, c_attn_w, c_attn_b, c_proj_w, c_proj_b, uk_w, uk_b, uv_w, uv_b):
        import jax, jax.numpy as jnp
        import numpy as np
        EMBED = 512
        HEADS = 16
        HDIM = EMBED // HEADS
        MASK_OUT = -10000.0

        def _split_heads(t):
            B, T, _ = t.shape
            return t.reshape(B, T, HEADS, HDIM).transpose(0, 2, 1, 3)
        B, S, _ = word_hidden_states.shape
        qkv = word_hidden_states @ c_attn_w + c_attn_b
        q_word, k_word, v_word = jnp.split(qkv, 3, axis=-1)
        img = image_hidden_states[:, None, :]
        k_img = img @ uk_w.T + uk_b
        v_img = img @ uv_w.T + uv_b
        k = jnp.concatenate([k_img, k_word], axis=1)
        v = jnp.concatenate([v_img, v_word], axis=1)
        q = _split_heads(q_word)
        k = _split_heads(k)
        v = _split_heads(v)
        scores = jnp.einsum('bhqd,bhkd->bhqk', q, k) / jnp.sqrt(jnp.float32(HDIM))
        qi = jnp.arange(S)[:, None]
        kj = jnp.arange(S + 1)[None, :]
        causal = kj <= qi + 1
        scores = jnp.where(causal[None, None], scores, jnp.float32(MASK_OUT))
        zero_col = jnp.zeros(attention_mask.shape[:-1] + (1,), attention_mask.dtype)
        mask = jnp.concatenate([zero_col, attention_mask], axis=-1)
        scores = scores + mask
        attn = jax.nn.softmax(scores, axis=-1)
        out = jnp.einsum('bhqk,bhkd->bhqd', attn, v)
        out = out.transpose(0, 2, 1, 3).reshape(B, S, EMBED)
        out = out @ c_proj_w + c_proj_b
        return out
    x = x + _L0_cond_ref(x, cond_1024, L0_cond_w_W, L0_cond_w_b, L0_cond_wx_W, L0_cond_wx_b, L0_cond_wh_W, L0_cond_wh_b)
    x = x + _L1_cond_ref(x, cond_1024, L1_cond_Wx, L1_cond_Wh, L1_cond_b)
    x = x + _L2_cond_ref(x, cond_1024, L2_cond_Wx, L2_cond_Wh, L2_cond_b)
    x = x + _L3_cond_ref(x, cond_1024, mask_Bx1x1xS_ff0, L3_cond_c_attn_w, L3_cond_c_attn_b, L3_cond_c_proj_w, L3_cond_c_proj_b, L3_cond_uk_w, L3_cond_uk_b, L3_cond_uv_w, L3_cond_uv_b)
    return x

_drawn_inputs = setup_inputs


def setup_inputs(seed=0):
    import zlib

    import numpy as np

    out = dict(_drawn_inputs(seed))
    spreads = {'L1_cond_b': (0.0, 0.1),
     'L2_cond_b': (0.0, 0.1),
     'L3_cond_c_attn_b': (0.0, 0.312),
     'L3_cond_c_proj_b': (0.0, 0.1),
     'L3_cond_uk_b': (0.0, 2.0),
     'L3_cond_uv_b': (0.0, 2.0)}
    factors = {'L0_cond_w_b': 22.825, 'L0_cond_wh_b': 4.94, 'L3_cond_uk_w': 8.0, 'L3_cond_uv_w': 8.0}
    for name, (base, spread) in spreads.items():
        noise = np.random.default_rng([zlib.crc32(name.encode()), seed]).standard_normal(out[name].shape)
        drawn = base * np.exp(spread * noise) if base else spread * noise
        out[name] = jnp.asarray(drawn.astype(out[name].dtype))
    for name, factor in factors.items():
        out[name] = (out[name] * factor).astype(out[name].dtype)
    return out
```

```python
from contextlib import ExitStack

import concourse.bass as bass
from concourse import mybir

F32 = mybir.dt.float32
ALU = mybir.AluOpType
ACT = mybir.ActivationFunctionType
AX = mybir.AxisListType

P = 128
B, T, D = 8, 512, 512
KC = D // P
CH = 16
NCH = T // CH
N = CH * B
ROUNDS = NCH + 4
G0 = 3 * KC
XW = G0 + KC
SLOTS = 2

BIAS_ROWS = [("w_b", 8), ("wh_b", 4), ("wx_b", 4), ("b1", 4), ("b2", 4),
             ("qkv_b", 12), ("proj_b", 4), ("uk_b", 4), ("uv_b", 4)]
BIAS_AT = {}
_at = 0
for _name, _n in BIAS_ROWS:
    BIAS_AT[_name] = _at
    _at += _n
NBIAS = _at


def fills_of(m):
    out = []
    if -1 <= m < NCH - 1:
        out += [(0, g) for g in range(G0)]
    if 0 <= m - 1 < NCH:
        out += [(1, g) for g in range(KC)]
    if 0 <= m - 3 < NCH:
        out += [(2, g) for g in range(KC)]
    return out


def plan(m):
    fills = fills_of(m)
    n = len(fills)
    by_step = [fills[n * s // CH:n * (s + 1) // CH] for s in range(CH)]
    chunk_ops = [[] for _ in range(CH)]
    if m < NCH - 1:
        chunk_ops[0].append(("stage", 0, m + 1))
    at = 1
    for layer, c in ((1, m - 1), (2, m - 3)):
        if 0 <= c < NCH:
            chunk_ops[at].append(("add", layer - 1, c))
            chunk_ops[at + 1].append(("stage", layer, c))
        at += 2
    if 0 <= m - 5 < NCH:
        chunk_ops[at].append(("add", 2, m - 5))
    layers = [l for l, c in ((0, m - 2), (1, m - 4)) if 0 <= c < NCH]
    return {"scan0": 0 <= m < NCH, "scan12": layers, "fills": by_step, "chunk_ops": chunk_ops}


class Mem:
    pass


def clear_signals(nc, mem):
    nc.all_engine_barrier(sems_to_clear=mem.sem_range)


def scan_rounds(nc, mem, sems, first, times):
    plans = [plan(first), plan(first + 1)]
    steps = [(u, t) for u in range(2) for t in range(CH)]
    S = len(steps)
    if times > 1:
        with nc.Fori(0, times) as i:
            scan_block(nc, mem, sems, plans, steps, S, first, i)
            clear_signals(nc, mem)
    else:
        scan_block(nc, mem, sems, plans, steps, S, first, None)
        clear_signals(nc, mem)


def scan_block(nc, mem, sems, plans, steps, S, first, i):
    s = sems
    X, stage, h0, h12, xw0, xw12 = mem.X, mem.stage, mem.h0, mem.h12, mem.xw0, mem.xw12

    def counts(per_step):
        out = [0]
        for u, t in steps:
            out.append(out[-1] + per_step(u, t))
        return out

    n0 = counts(lambda u, t: int(plans[u]["scan0"]))
    n12 = counts(lambda u, t: int(bool(plans[u]["scan12"])))
    nfill = counts(lambda u, t: len(plans[u]["fills"][t]))
    nchunk = counts(lambda u, t: len(plans[u]["chunk_ops"][t]))
    staged = {}
    q = 0
    for u, t in steps:
        for kind, layer, c in plans[u]["chunk_ops"][t]:
            q += 1
            if kind == "stage":
                staged[u, layer] = q
    last_fill = {}
    q = 0
    for u, t in steps:
        for layer, g in plans[u]["fills"][t]:
            q += 1
            last_fill[u, layer] = q
    half = nfill[CH]

    def before(u, t):
        return (u, t - 1) if t else (1 - u, CH - 1)

    with nc.Block(no_gpsimd_drain=True) as block:

        @block.tensor
        def _(pe):
            def main0(n, u, t):
                if n0[n]:
                    pe.wait_ge(s.h0_new, n0[n])
                us, ts = before(u, t)
                for k in range(KC):
                    for j in range(KC):
                        mm = pe.matmul(mem.ps0[32 * j:32 * j + B, 0:G0 // KC * P],
                                       h0[:, us, k, ts, :], mem.wh0[:, k, j, :],
                                       start=(k == 0), stop=(k == KC - 1))
                mm.then_inc(s.main0_done, 1)

            def main12(n, u, t, ks):
                if n12[n] and ks[0] == 0:
                    pe.wait_ge(s.h12_new, n12[n])
                us, ts = before(u, t)
                for k in ks:
                    for l in plans[u]["scan12"]:
                        for j in range(2):
                            at = 32 * (2 * l + j)
                            mm = pe.matmul(mem.ps12[at:at + B, 0:2 * P],
                                           h12[:, us, l, k, ts, :],
                                           mem.wh12[:, l, k, 2 * P * j:2 * P * (j + 1)],
                                           start=(k == 0), stop=(k == KC - 1))
                if ks[-1] == KC - 1:
                    mm.then_inc(s.main12_done, 1)

            fill = 0
            for n, (u, t) in enumerate(steps):
                p = plans[u]
                if p["scan0"]:
                    main0(n, u, t)
                if p["scan12"]:
                    main12(n, u, t, (0, 1))
                if p["scan0"]:
                    pe.wait_ge(s.rows0_copied, n0[n] + 1)
                    for g in range(G0 // KC):
                        mm = pe.transpose(mem.tp0[:, g * P:(g + 1) * P],
                                          mem.rows0[:, g * P:(g + 1) * P], mem.ident[:, :])
                    mm.then_inc(s.turned0, 1)
                if p["scan12"]:
                    main12(n, u, t, (2, 3))
                for layer, g in p["fills"][t]:
                    pe.wait_ge(s.chunk_op, staged[u, layer])
                    if fill >= 2:
                        pe.wait_ge(s.fill_kept, fill - 1)
                    w = mem.wx[layer]
                    for k in range(KC):
                        mm = pe.matmul(mem.fillps[fill % 2][:, 0:N], w[:, k, g * P:(g + 1) * P],
                                       stage[layer][:, k, :], start=(k == 0), stop=(k == KC - 1))
                    mm.then_inc(s.fill_done, 1)
                    fill += 1
                if p["scan12"]:
                    pe.wait_ge(s.rows12_copied, n12[n] + 1)
                    for g in range(2):
                        mm = pe.transpose(mem.tp12[:, g * P:(g + 1) * P],
                                          mem.rows12[:, g * P:(g + 1) * P], mem.ident[:, :])
                    mm.then_inc(s.turned12, 1)

        @block.scalar
        def _(act):
            def tanh12(n, u, t):
                act.wait_ge(s.pre12, n12[n] + 1)
                ls = plans[u]["scan12"]
                l0, l1 = 2 * ls[0], 2 * ls[-1] + 2
                nc.scalar.activation(
                    h12[:, u, :, :, t, :].rearrange("p l (j g) b -> p g (l j) b", g=2)[:, :, l0:l1, :],
                    mem.sum12[:, :, l0:l1, :], ACT.Tanh).then_inc(s.h12_new, 1)

            for n, (u, t) in enumerate(steps):
                p = plans[u]
                if n:
                    v, w = steps[n - 1]
                    if plans[v]["scan12"]:
                        tanh12(n - 1, v, w)
                if n == CH and p["scan12"] and nchunk[CH]:
                    act.wait_ge(s.chunk_op, nchunk[CH])
                if p["scan0"]:
                    act.wait_ge(s.main0_done, n0[n] + 1)
                    nc.scalar.copy(mem.rows0[:, :], mem.ps0[:, 0:G0 // KC * P]).then_inc(s.rows0_copied, 1)
                    act.wait_ge(s.pre0, n0[n] + 1)
                    nc.scalar.activation(mem.gates0[:, :, :], mem.pre0[:, 0:2 * KC, :],
                                         ACT.Sigmoid).then_inc(s.gates0, 1)
                    act.wait_ge(s.memory0, n0[n] + 1)
                    nc.scalar.activation(mem.tanh0[:, :, :], mem.mem0[:, :, :],
                                         ACT.Tanh).then_inc(s.tanh0, 1)
                if p["scan12"]:
                    act.wait_ge(s.main12_done, n12[n] + 1)
                    nc.scalar.copy(mem.rows12[:, :], mem.ps12[:, 0:2 * P]).then_inc(s.rows12_copied, 1)
            u, t = steps[-1]
            if plans[u]["scan12"]:
                tanh12(S - 1, u, t)

        @block.vector
        def _(dve):
            kept = [0]

            def pre12(n, u, t):
                ls = plans[u]["scan12"]
                l0, l1 = 2 * ls[0], 2 * ls[-1] + 2
                dve.wait_ge(s.turned12, n12[n] + 1)
                nc.vector.tensor_tensor(
                    mem.sum12[:, :, l0:l1, :],
                    mem.tp12[:, 0:2 * P].rearrange("p (g j c) -> p g j c", g=2, j=4)[:, :, l0:l1, 0:B],
                    xw12[:, u, :, :, t, :].rearrange("p l (j g) b -> p g (l j) b", g=2)[:, :, l0:l1, :],
                    ALU.add).then_inc(s.pre12, 1)

            def keep_fills(u, t):
                for layer, g in plans[u]["fills"][t]:
                    kept[0] += 1
                    dve.wait_ge(s.fill_done, kept[0])
                    if layer == 0:
                        at = g if g < 2 * KC else g + KC
                        dst = xw0[:, 1 - u, at, :, :]
                        bias = BIAS_AT["w_b"] + g if g < 2 * KC else BIAS_AT["wx_b"] + g - 2 * KC
                    else:
                        dst = xw12[:, 1 - u, layer - 1, g, :, :]
                        bias = BIAS_AT[f"b{layer}"] + g
                    nc.vector.tensor_scalar(
                        dst, mem.fillps[(kept[0] - 1) % 2][:, 0:N].rearrange("p (t b) -> p t b", b=B),
                        mem.biasT[:, bias:bias + 1], None, ALU.add).then_inc(s.fill_kept, 1)

            for n, (u, t) in enumerate(steps):
                p = plans[u]
                if n:
                    v, w = steps[n - 1]
                    if plans[v]["scan12"]:
                        pre12(n - 1, v, w)
                    keep_fills(v, w)
                if n == CH and half:
                    dve.wait_ge(s.fill_kept, half)
                if p["scan0"]:
                    dve.wait_ge(s.turned0, n0[n] + 1)
                    nc.vector.tensor_tensor(
                        mem.pre0[:, :, :],
                        mem.tp0[:, 0:G0 // KC * P].rearrange("p (g c) -> p g c", c=32)[:, :, 0:B],
                        xw0[:, u, 0:G0, t, :], ALU.add).then_inc(s.pre0, 1)
                    dve.wait_ge(s.gates0, n0[n] + 1)
                    nc.vector.tensor_tensor(mem.gated0[:, :, :], mem.gates0[:, 0:KC, :],
                                            mem.pre0[:, 2 * KC:G0, :], ALU.mult).then_inc(s.gated0, 1)
                    dve.wait_ge(s.gated0, n0[n] + 1)
                    nc.vector.tensor_tensor(mem.mem0[:, :, :], mem.gated0[:, :, :],
                                            xw0[:, u, G0:XW, t, :], ALU.add).then_inc(s.memory0, 1)
                    dve.wait_ge(s.tanh0, n0[n] + 1)
                    dve.wait_ge(s.blend0, 2 * n0[n] + 2)
                    nc.vector.tensor_tensor(mem.fresh0[:, :, :], mem.keep0[:, :, :],
                                            mem.tanh0[:, :, :], ALU.mult).then_inc(s.fresh0, 1)
                    dve.wait_ge(s.fresh0, n0[n] + 1)
                    nc.vector.tensor_tensor(h0[:, u, :, t, :], mem.fresh0[:, :, :],
                                            mem.held0[:, :, :], ALU.add).then_inc(s.h0_new, 1)
            u, t = steps[-1]
            if plans[u]["scan12"]:
                pre12(S - 1, u, t)
            keep_fills(u, t)

        @block.gpsimd
        def _(pool):
            def x_chunk(c):
                if i is None:
                    return X[:, :, :, c * CH:(c + 1) * CH]
                return X[:, :, :, bass.ds(i * (2 * CH) + c * CH, CH)]

            done = 0
            for n, (u, t) in enumerate(steps):
                p = plans[u]
                for kind, layer, c in p["chunk_ops"][t]:
                    if kind == "stage":
                        if done:
                            pool.wait_ge(s.chunk_op, done)
                        if u and (0, layer) in last_fill:
                            pool.wait_ge(s.fill_done, last_fill[0, layer])
                        nc.gpsimd.tensor_copy(
                            stage[layer][:, :, :].rearrange("p k (t b) -> p k b t", b=B),
                            x_chunk(c)).then_inc(s.chunk_op, 1)
                    else:
                        if u:
                            if layer == 0:
                                pool.wait_ge(s.h0_new, n0[CH])
                            else:
                                pool.wait_ge(s.h12_new, n12[CH])
                        ring = h0[:, 1 - u, :, :, :] if layer == 0 else h12[:, 1 - u, layer - 1, :, :, :]
                        nc.gpsimd.tensor_tensor(x_chunk(c), x_chunk(c),
                                                ring.rearrange("p k t b -> p k b t"),
                                                ALU.add).then_inc(s.chunk_op, 1)
                    done += 1
                if p["scan0"]:
                    us, ts = before(u, t)
                    if n0[n]:
                        pool.wait_ge(s.h0_new, n0[n])
                    pool.wait_ge(s.gates0, n0[n] + 1)
                    nc.gpsimd.tensor_scalar(mem.keep0[:, :, :], mem.gates0[:, KC:2 * KC, :],
                                            -1.0, 1.0, ALU.mult, ALU.add).then_inc(s.blend0, 1)
                    nc.gpsimd.tensor_tensor(mem.held0[:, :, :], mem.gates0[:, KC:2 * KC, :],
                                            h0[:, us, :, ts, :], ALU.mult).then_inc(s.blend0, 1)


def add_last_chunk(nc, mem):
    with nc.Block(no_gpsimd_drain=True) as block:

        @block.gpsimd
        def _(pool):
            last = mem.X[:, :, :, T - CH:T]
            nc.gpsimd.tensor_tensor(last, last,
                                    mem.h12[:, (NCH - 1) % 2, 1, :, :, :].rearrange("p k t b -> p k b t"), ALU.add)


def setup(nc, mem, sems, a):
    s = sems
    NT = T // P
    tiles = [(b, tc) for b in range(B) for tc in range(NT)]
    loads = []
    for k in range(KC):
        rows = slice(k * P, (k + 1) * P)
        hrows = slice(D + k * P, D + (k + 1) * P)
        for g, src in enumerate((a["w_W"][hrows, 0:D], a["w_W"][hrows, D:2 * D], a["wh_W"][rows, :])):
            loads.append((mem.wh0[:, k, :, g * P:(g + 1) * P], src.rearrange("p (j c) -> p j c", c=P)))
        loads.append((mem.wx[0][:, k, 0:2 * D], a["w_W"][rows, :]))
        loads.append((mem.wx[0][:, k, 2 * D:3 * D], a["wx_W"][rows, :]))
    for l in (1, 2):
        loads.append((mem.wx[l][:, :, :], a[f"L{l}_Wx"].rearrange("(k p) n -> p k n", p=P)))
        loads.append((mem.wh12[:, l - 1, :, :], a[f"L{l}_Wh"].rearrange("(k p) n -> p k n", p=P)))
    names = {"w_b": "w_b", "wh_b": "wh_b", "wx_b": "wx_b", "b1": "L1_b", "b2": "L2_b",
             "qkv_b": "qkv_b", "proj_b": "proj_b", "uk_b": "uk_b", "uv_b": "uv_b"}
    XR = 4

    with nc.Block(no_gpsimd_drain=True) as block:

        @block.sync
        def _(sp):
            sp.dma_start(mem.cond_rows[0:B, :], a["cond"]).then_inc(s.small_in, 16)
            for name, n in BIAS_ROWS:
                at = BIAS_AT[name]
                sp.dma_start(mem.bias_rows[at:at + n, :],
                             a[names[name]].rearrange("(r c) -> r c", c=P)).then_inc(s.small_in, 16)
            for q, (b, tc) in enumerate(tiles):
                if q >= XR:
                    sp.wait_ge(s.x_turned, q - XR + 1)
                sp.dma_start(mem.xrows[:, q % XR, :],
                             a["x"][b, tc * P:(tc + 1) * P, :]).then_inc(s.x_in[q % XR], 16)

        @block.scalar
        def _(act):
            for dst, src in loads:
                act.dma_start(dst, src).then_inc(s.weights_in, 16)
            for q, (b, tc) in enumerate(tiles):
                if q % 2:
                    act.wait_ge(s.x_turned, q + 1)
                    nc.scalar.copy(mem.X[:, :, b, tc * P:(tc + 1) * P],
                                   mem.xps[q % 2][:, :].rearrange("p (k t) -> p k t", k=KC)).then_inc(s.x_kept1, 1)
            act.wait_ge(s.weights_in, 16 * len(loads))

        @block.gpsimd
        def _(pool):
            nc.gpsimd.memset(mem.ident[:, :], 0.0).then_inc(s.ident, 1)
            pool.wait_ge(s.ident, 1)
            nc.gpsimd.affine_select(out=mem.ident[:, :], in_=mem.ident[:, :], compare_op=ALU.not_equal,
                                    fill=1.0, base=0, pattern=[[-1, P]],
                                    channel_multiplier=1).then_inc(s.ident, 1)
            nc.gpsimd.memset(mem.xw0[:, :, G0 - KC:G0, :, :], 0.0).then_inc(s.zeroed, 1)
            pool.wait_ge(s.x_kept0, len(tiles) // 2)
            pool.wait_ge(s.x_kept1, len(tiles) // 2)
            nc.gpsimd.tensor_copy(mem.stage[0][:, :, :].rearrange("p k (t b) -> p k b t", b=B),
                                  mem.X[:, :, :, 0:CH]).then_inc(s.chunk_op, 1)

        @block.tensor
        def _(pe):
            pe.wait_ge(s.ident, 2)
            pe.wait_ge(s.small_in, 16 * (1 + len(BIAS_ROWS)))
            for k in range(KC):
                pe.transpose(mem.fillps[0][:, B * k:B * (k + 1)],
                             mem.cond_rows[0:B, k * P:(k + 1) * P], mem.ident[0:B, 0:B])
            pe.transpose(mem.fillps[1][:, 0:NBIAS], mem.bias_rows[0:NBIAS, :],
                         mem.ident[0:NBIAS, 0:NBIAS]).then_inc(s.small_turned, 1)
            for q in range(len(tiles)):
                pe.wait_ge(s.x_in[q % XR], 16 * (q // XR + 1))
                if q >= 2:
                    pe.wait_ge(s.x_kept0 if q % 2 == 0 else s.x_kept1, q // 2)
                for k in range(KC):
                    mm = pe.transpose(mem.xps[q % 2][:, k * P:(k + 1) * P],
                                      mem.xrows[:, q % XR, k * P:(k + 1) * P], mem.ident[:, :])
                mm.then_inc(s.x_turned, 1)
            pe.wait_ge(s.weights_in, 16 * len(loads))
            pe.wait_ge(s.chunk_op, 1)
            pe.wait_ge(s.small_kept, 1)
            for f, (layer, g) in enumerate(fills_of(-1)):
                if f >= 2:
                    pe.wait_ge(s.fill_kept, f - 1)
                for k in range(KC):
                    mm = pe.matmul(mem.fillps[f % 2][:, 0:N], mem.wx[0][:, k, g * P:(g + 1) * P],
                                   mem.stage[0][:, k, :], start=(k == 0), stop=(k == KC - 1))
                mm.then_inc(s.fill_done, 1)

        @block.vector
        def _(dve):
            nc.vector.memset(mem.ps0[:, :], 0.0)
            nc.vector.memset(mem.ps12[:, :], 0.0)
            dve.wait_ge(s.small_turned, 1)
            nc.vector.tensor_copy(mem.biasT[:, :], mem.fillps[1][:, 0:NBIAS]).then_inc(s.bias_kept, 1)
            cond = mem.fillps[0][:, 0:B * KC].rearrange("p (k b) -> p k b", b=B)
            nc.vector.tensor_copy(mem.h0[:, 1, :, CH - 1, :], cond)
            nc.vector.tensor_copy(mem.h12[:, 1, 0, :, CH - 1, :], cond)
            nc.vector.tensor_copy(mem.h12[:, 1, 1, :, CH - 1, :], cond)
            nc.vector.tensor_copy(mem.condT[:, :, :], cond).then_inc(s.small_kept, 1)
            dve.wait_ge(s.bias_kept, 1)
            dve.wait_ge(s.zeroed, 1)
            for slot in range(SLOTS):
                for g in range(KC):
                    at = BIAS_AT["wh_b"] + g
                    addend = mem.xw0[:, slot, G0 - KC + g, :, :]
                    nc.vector.tensor_scalar(addend, addend, mem.biasT[:, at:at + 1], None, ALU.add)
            for q, (b, tc) in enumerate(tiles):
                if q % 2 == 0:
                    dve.wait_ge(s.x_turned, q + 1)
                    nc.vector.tensor_copy(mem.X[:, :, b, tc * P:(tc + 1) * P],
                                          mem.xps[q % 2][:, :].rearrange("p (k t) -> p k t", k=KC)).then_inc(s.x_kept0, 1)
            for f, (layer, g) in enumerate(fills_of(-1)):
                dve.wait_ge(s.fill_done, f + 1)
                at = g if g < 2 * KC else g + KC
                bias = BIAS_AT["w_b"] + g if g < 2 * KC else BIAS_AT["wx_b"] + g - 2 * KC
                nc.vector.tensor_scalar(mem.xw0[:, 0, at, :, :],
                                        mem.fillps[f % 2][:, 0:N].rearrange("p (t b) -> p t b", b=B),
                                        mem.biasT[:, bias:bias + 1], None, ALU.add).then_inc(s.fill_kept, 1)


HG = 4
HPG = 4
HD = P // HPG
QC = T // P
UNITS = HG * QC
RING = 3
LAG = 2
PER_TURN = [4, 2, 1, 1]
TURNS = [HPG // n + 1 for n in PER_TURN]
EXTRAS = 2
FAR = 32
MASK_OUT = -10000.0
FAR_DOWN = -1.0e30
LOWEST = -3.0e38
TRI = [0, P, 3 * P, 6 * P, 10 * P]


def attention_setup(nc, mem, sems, a):
    s = sems
    uk_rows, uv_rows = mem.probsT[:, 0, :, :], mem.probsT[:, 1, :, :]
    ukT, uvT = mem.probsT[:, 2, :, :], mem.probsT[:, 3, :, :]
    turns = [(rows, dst, o, k) for rows, dst in ((uk_rows, ukT), (uv_rows, uvT)) for k in range(KC) for o in range(KC)]
    NTURN = len(turns) // KC

    with nc.Block(no_gpsimd_drain=True) as block:

        @block.sync
        def _(sp):
            sp.dma_start(uk_rows, a["uk_w"].rearrange("(o p) n -> p o n", p=P)).then_inc(s.image_in, 16)
            sp.dma_start(uv_rows, a["uv_w"].rearrange("(o p) n -> p o n", p=P)).then_inc(s.image_in, 16)
            sp.dma_start(mem.row_biases[0:1, 0, :],
                         a["qkv_b"][2 * D:3 * D].rearrange("(o n) -> o n", o=1)).then_inc(s.small_in, 16)
            sp.dma_start(mem.row_biases[0:1, 1, :],
                         a["proj_b"].rearrange("(o n) -> o n", o=1)).then_inc(s.small_in, 16)
            sp.dma_start(mem.w_qkv[:, :, :], a["qkv_w"].rearrange("(k p) n -> p k n", p=P)).then_inc(s.weights_in, 16)
            sp.dma_start(mem.w_proj[:, :, :], a["proj_w"].rearrange("(k p) n -> p k n", p=P)).then_inc(s.weights_in, 16)
            sp.wait_ge(s.weights_in, 32)

        @block.gpsimd
        def _(pool):
            nc.gpsimd.memset(mem.ones[:, :], 1.0).then_inc(s.ident, 1)
            nc.gpsimd.memset(mem.drop_masked[:, :], 0.0).then_inc(s.zeroed, 1)
            nc.gpsimd.memset(mem.drop_kept[:, :], LOWEST).then_inc(s.zeroed, 1)
            pool.wait_ge(s.zeroed, 2)
            nc.gpsimd.affine_select(out=mem.drop_masked[:, :], in_=mem.drop_masked[:, :],
                                    compare_op=ALU.is_ge, fill=FAR_DOWN, base=0,
                                    pattern=[[-1, P]], channel_multiplier=1).then_inc(s.zeroed, 1)
            nc.gpsimd.affine_select(out=mem.drop_kept[:, :], in_=mem.drop_kept[:, :],
                                    compare_op=ALU.is_ge, fill=0.0, base=0,
                                    pattern=[[-1, P]], channel_multiplier=1).then_inc(s.zeroed, 1)
            nc.gpsimd.memset(mem.probs_extra[:, :], 0.0)
            nc.gpsimd.memset(mem.head_wide[:, :], 0.0).then_inc(s.head_wide, 1)
            nc.gpsimd.memset(mem.k_image[:, :, :, :], 0.0).then_inc(s.image_zero, 1)
            nc.gpsimd.memset(mem.v_image[:, :, :, :], 0.0).then_inc(s.image_zero, 1)

        @block.tensor
        def _(pe):
            pe.wait_ge(s.ident, 1)
            pe.wait_ge(s.small_in, 32)
            for q in range(2):
                mm = pe.matmul(mem.banks[q][:, :], mem.ones[0:1, :], mem.row_biases[0:1, q, :],
                               start=True, stop=True)
            mm.then_inc(s.rows_made, 1)
            pe.wait_ge(s.head_wide, 2)
            pe.transpose(mem.banks[6][:, 0:P], mem.head_wide[:, :], mem.ident[:, :]).then_inc(s.head_turned, 1)
            pe.wait_ge(s.image_in, 32)
            for q in range(NTURN):
                if q >= 2:
                    pe.wait_ge(s.turn_kept, q - 1)
                for r in range(KC):
                    rows, dst, o, k = turns[q * KC + r]
                    mm = pe.transpose(mem.banks[2 + q % 2][:, o * P:(o + 1) * P],
                                      rows[:, o, k * P:(k + 1) * P], mem.ident[:, :])
                mm.then_inc(s.turned, 1)
            pe.wait_ge(s.turn_kept, NTURN)
            for q, wT in enumerate((ukT, uvT)):
                for o in range(KC):
                    for k in range(KC):
                        mm = pe.matmul(mem.banks[4 + q][:, B * o:B * (o + 1)],
                                       wT[:, k, o * P:(o + 1) * P], mem.condT[:, k, :],
                                       start=(k == 0), stop=(k == KC - 1))
            mm.then_inc(s.image_made, 1)

        @block.vector
        def _(dve):
            nc.vector.memset(mem.head_rows[:, :], 0.0).then_inc(s.head_zero, 1)
            dve.wait_ge(s.head_zero, 1)
            dve.wait_ge(s.head_wide, 1)
            for g in range(HPG):
                nc.vector.memset(mem.head_rows[HD * g:HD * (g + 1), g:g + 1], 1.0)
                ins = nc.vector.memset(mem.head_wide[HD * g:HD * (g + 1), :].rearrange("p (q c) -> p q c", q=QC)[:, :, EXTRAS * g], 1.0)
            ins.then_inc(s.head_wide, 1)
            nc.vector.memset(mem.tail_sum[:, :], 0.0)
            dve.wait_ge(s.head_turned, 1)
            nc.vector.tensor_copy(mem.head_block[:, :], mem.banks[6][:, 0:P])
            dve.wait_ge(s.rows_made, 1)
            for q in range(2):
                nc.vector.tensor_copy(mem.bias_tiles[:, q, :], mem.banks[q][:, :])
            for q in range(NTURN):
                dve.wait_ge(s.turned, q + 1)
                _, dst, _, k = turns[q * KC]
                nc.vector.tensor_copy(dst[:, k, :], mem.banks[2 + q % 2][:, :]).then_inc(s.turn_kept, 1)
            dve.wait_ge(s.image_made, 1)
            dve.wait_ge(s.image_zero, 2)
            for q, (dst, name) in enumerate(((mem.k_image, "uk_b"), (mem.v_image, "uv_b"))):
                for hg in range(HG):
                    for g in range(HPG):
                        rows = slice(HD * g, HD * (g + 1))
                        col = BIAS_AT[name] + hg
                        nc.vector.tensor_scalar(dst[rows, :, hg, g], mem.banks[4 + q][rows, B * hg:B * (hg + 1)],
                                                mem.biasT[rows, col:col + 1], None, ALU.add)
            at = BIAS_AT["qkv_b"]
            nc.vector.tensor_scalar(mem.q_bias[:, :], mem.biasT[:, at:at + HG], HD ** -0.5, None, ALU.mult)


def attention_batch(nc, mem, sems, a, out, b):
    s = sems
    units = [(hg, qc) for hg in range(HG) for qc in range(QC)]

    at_start = [("k", 0), ("q", 0), ("image", 0)]
    at_step = {i: [] for i in range(UNITS)}
    for qc in range(QC):
        at_step[qc].append(("v", qc))
    at_step[QC].append(("hidden", 0))
    for hg in range(1, HG):
        at_step[QC * hg - 3].append(("k", hg))
        at_step[QC * hg - 1].append(("q", hg))
    ahead = {i: [("image", units[i][0])] if i and units[i][1] == 0 else [] for i in range(UNITS)}
    turned_by = [0]
    for _, qc in units:
        turned_by.append(turned_by[-1] + TURNS[qc])
    place = {}
    for job in at_start + [job for i in range(UNITS) for job in ahead[i] + at_step[i]]:
        place[job] = len(place)

    def group_ended(i):
        v = i - LAG
        return units[v][0] if 0 <= v < UNITS and units[v][1] == QC - 1 else None

    with nc.Block(no_gpsimd_drain=True) as block:

        @block.sync
        def _(sp):
            sp.dma_start(mem.mask_row[0:1, :], a["mask"][bass.ds(b, 1), :]).then_inc(s.small_in, 16)
            for tc in range(QC):
                sp.wait_ge(s.out_rows, tc + 1)
                sp.dma_start(out[bass.ds(b, 1), tc * P:(tc + 1) * P, :].rearrange("o t n -> (o t) n"),
                             mem.out_rows[:, tc % 2, :]).then_inc(s.out_sent[tc % 2], 16)
            sp.wait_ge(s.out_sent[0], 16 * QC // 2)
            sp.wait_ge(s.out_sent[1], 16 * QC // 2)

        @block.tensor
        def _(pe):
            def product(kind, c):
                bank = mem.banks[6]
                n = place[kind, c]
                if n:
                    pe.wait_ge(s.product_kept, n)
                if kind == "image":
                    for qc in range(QC):
                        mm = pe.matmul(bank[:, HPG * qc:HPG * (qc + 1)],
                                       mem.qT[:, qc * P:(qc + 1) * P], mem.k_image_b[:, c, :],
                                       start=True, stop=True)
                elif kind == "hidden":
                    for kc in range(1, QC):
                        mm = pe.matmul(bank[:, :], mem.hidden_w[:, kc - 1, :], mem.v[:, kc, :],
                                       start=(kc == 1), stop=(kc == QC - 1))
                elif kind == "v":
                    for k in range(KC):
                        mm = pe.matmul(bank[:, :], mem.xT[:, k, c * P:(c + 1) * P],
                                       mem.w_qkv[:, k, 2 * D:3 * D], start=(k == 0), stop=(k == KC - 1))
                else:
                    at = (0 if kind == "q" else D) + c * P
                    for k in range(KC):
                        mm = pe.matmul(bank[:, :], mem.w_qkv[:, k, at:at + P],
                                       mem.X[:, k, bass.ds(b, 1), :].rearrange("p o t -> p (o t)"),
                                       start=(k == 0), stop=(k == KC - 1))
                mm.then_inc(s.product_done, 1)

            def scores(i):
                hg, qc = units[i]
                n = P * (qc + 1)
                pe.wait_ge(s.queries_alone, i + 1)
                for g in range(HPG):
                    if i:
                        pe.wait_ge(s.scores_read, HPG * (i - 1) + g + 1)
                    pe.matmul(mem.banks[g][:, 0:n], mem.q_alone[:, i % 2, g, :],
                              mem.kT[:, hg % 2, 0:n], start=True, stop=True).then_inc(s.scores_done, 1)

            def turn(v):
                qc = units[v][1]
                n, per = qc + 1, PER_TURN[qc]
                for r in range(TURNS[qc]):
                    q = turned_by[v] + r
                    if q >= 2:
                        pe.wait_ge(s.turn_kept, q - 1)
                    bank = mem.banks[4 + q % 2]
                    if r < HPG // per:
                        for h in range(per):
                            g = per * r + h
                            pe.wait_ge(s.probs_ready, HPG * v + g + 1)
                            for kc in range(n):
                                at = EXTRAS + kc * P
                                mm = pe.transpose(bank[:, (h * n + kc) * P:(h * n + kc + 1) * P],
                                                  mem.probs[:, v % RING, g, at:at + P], mem.ident[:, :])
                    else:
                        mm = pe.matmul(bank[FAR * qc:FAR * qc + EXTRAS * HPG, 0:P],
                                       mem.extras[:, v % RING, :], mem.ident[:, :], start=True, stop=True)
                    mm.then_inc(s.turned, 1)

            def weigh(hg):
                pe.wait_ge(s.turn_kept, turned_by[QC * (hg + 1)])
                if hg == 0:
                    pe.wait_ge(s.product_kept, place["hidden", 0] + 1)
                else:
                    pe.wait_ge(s.weighed_kept, hg)
                pe.matmul(mem.banks[7][:, :], mem.v_extra[:, hg, :], mem.probs_extra[:, :],
                          start=True, stop=False, skip_group_check=True)
                for kc in range(QC):
                    for g in range(HPG):
                        at = HD * (HPG * hg + g)
                        mm = pe.matmul(mem.banks[7][HD * g:HD * (g + 1), kc * P:T], mem.v[:, kc, at:at + HD],
                                       mem.probsT[:, g, kc, kc * P:T], start=False, stop=(kc == QC - 1),
                                       skip_group_check=True)
                mm.then_inc(s.weighed, 1)

            pe.wait_ge(s.small_in, 16)
            pe.matmul(mem.banks[7][:, :], mem.ones[0:1, :], mem.mask_row[0:1, :],
                      start=True, stop=True)
            for kc in range(QC):
                mm = pe.matmul(mem.banks[4][:, kc:kc + 1], mem.mask_row[0:1, kc * P:(kc + 1) * P],
                               mem.ones[0:1, 0:1], start=True, stop=True)
            mm.then_inc(s.rows_made, 1)
            pe.wait_ge(s.image_b, 2)
            for hg in range(HG):
                mm = pe.transpose(mem.banks[5][:, hg * P:(hg + 1) * P], mem.v_image_wide[:, hg, :], mem.ident[:, :])
            mm.then_inc(s.image_made, 1)
            for job in at_start:
                product(*job)
            pe.wait_ge(s.x_in_place, 1)
            pe.wait_ge(s.addends_ready, 1)
            pe.wait_ge(s.image_kept, 1)
            for i in range(UNITS + LAG + 1):
                if i < UNITS:
                    for job in ahead[i]:
                        product(*job)
                    scores(i)
                if group_ended(i - 1) is not None:
                    weigh(group_ended(i - 1))
                if i < UNITS:
                    for job in at_step[i]:
                        product(*job)
                if LAG <= i < UNITS + LAG:
                    turn(i - LAG)
            pe.wait_ge(s.weighed_kept, HG)
            for tc in range(QC):
                for k in range(KC):
                    pe.matmul(mem.banks[tc][:, :], mem.attnT[:, k, tc * P:(tc + 1) * P],
                              mem.w_proj[:, k, :], start=(k == 0), stop=False, skip_group_check=True)
                for k in range(KC):
                    mm = pe.matmul(mem.banks[tc][:, k * P:(k + 1) * P], mem.xT[:, k, tc * P:(tc + 1) * P],
                                   mem.ident[:, :], start=False, stop=(k == KC - 1), skip_group_check=True)
                mm.then_inc(s.projected, 1)

        @block.scalar
        def _(act):
            def exps(i):
                n = P * (units[i][1] + 1)
                act.wait_ge(s.maxima_ready, i + 1)
                nc.scalar.activation(mem.probs[:, i % RING, :, 0], mem.neg_max[:, i % RING, :], ACT.Exp,
                                     bias=mem.masked_max[:, 0:1])
                for g in range(HPG):
                    row = mem.probs[:, i % RING, g, 1:EXTRAS + n]
                    nc.scalar.activation(row, row, ACT.Exp, bias=mem.neg_max[:, i % RING, g:g + 1],
                                         accum_out=mem.sums[:, i % RING, g:g + 1]).then_inc(s.exps_done, 1)

            def keep_turn(v):
                hg, qc = units[v]
                if qc == 0 and hg:
                    act.wait_ge(s.weighed, hg)
                n, per = qc + 1, PER_TURN[qc]
                for r in range(TURNS[qc]):
                    q = turned_by[v] + r
                    act.wait_ge(s.turned, q + 1)
                    bank = mem.banks[4 + q % 2]
                    if r < HPG // per:
                        nc.scalar.copy(mem.probsT[:, per * r:per * (r + 1), 0:n, qc * P:(qc + 1) * P],
                                       bank[:, 0:per * n * P].rearrange("p (h k q) -> p h k q", h=per, k=n)).then_inc(s.turn_kept, 1)
                    else:
                        rows = slice(FAR * qc, FAR * qc + EXTRAS * HPG)
                        nc.scalar.copy(mem.probs_extra[rows, qc * P:(qc + 1) * P],
                                       bank[rows, 0:P]).then_inc(s.turn_kept, 1)

            act.wait_ge(s.masked_ready, 1)
            for qc in range(QC - 1):
                nc.scalar.activation(mem.hidden_rows[:, qc, (qc + 1) * P:T], mem.masked_all[:, (qc + 1) * P:T], ACT.Exp,
                                     bias=mem.neg_masked[:, 0:1], accum_out=mem.tail_sum[:, qc:qc + 1])
            nc.scalar.activation(mem.hidden_col[:, :], mem.masked_col[:, :], ACT.Exp,
                                 bias=mem.neg_masked[:, 0:1]).then_inc(s.hidden_exp, 1)
            for i in range(UNITS + LAG):
                if 1 <= i <= UNITS:
                    exps(i - 1)
                if i >= LAG:
                    keep_turn(i - LAG)

        @block.vector
        def _(dve):
            def keep(kind, c):
                dve.wait_ge(s.product_done, place[kind, c] + 1)
                bank = mem.banks[6]
                if kind == "k":
                    col = BIAS_AT["qkv_b"] + HG + c
                    ins = nc.vector.tensor_scalar(mem.kT[:, c % 2, :], bank[:, :], mem.biasT[:, col:col + 1],
                                                  None, ALU.add)
                elif kind == "q":
                    if c:
                        dve.wait_ge(s.queries_alone, QC * c)
                    ins = nc.vector.tensor_scalar(mem.qT[:, :], bank[:, :], HD ** -0.5,
                                                  mem.q_bias[:, c:c + 1], ALU.mult, ALU.add)
                elif kind == "v":
                    ins = nc.vector.tensor_tensor(mem.v[:, c, :], bank[:, :], mem.bias_tiles[:, 0, :], ALU.add)
                elif kind == "hidden":
                    nc.vector.tensor_tensor(mem.hidden_v[:, :].rearrange("p (h c) -> p h c", h=HG),
                                            bank[:, :].rearrange("p (h c) -> p h c", h=HG),
                                            mem.head_block[:, :].unsqueeze(1).to_broadcast([P, HG, P]),
                                            ALU.mult).then_inc(s.hidden_v, 1)
                    dve.wait_ge(s.hidden_v, 1)
                    ins = nc.vector.tensor_tensor(mem.v_extra[:, :, :], mem.v_extra[:, :, :],
                                                  mem.hidden_v[:, :].rearrange("p (h c) -> p h c", h=HG), ALU.add)
                else:
                    ins = nc.vector.tensor_copy(mem.image_scores[:, c % 2, :], bank[:, 0:HPG * QC])
                ins.then_inc(s.product_kept, 1)

            def scores_of(i):
                hg, qc = units[i]
                n = P * (qc + 1)
                slot = i % RING
                if i >= RING:
                    dve.wait_ge(s.turned, turned_by[i - RING + 1])
                for g in range(HPG):
                    dve.wait_ge(s.scores_done, HPG * i + g + 1)
                    nc.vector.tensor_tensor_reduce(
                        out=mem.probs[:, slot, g, EXTRAS:EXTRAS + n], in0=mem.banks[g][:, 0:n],
                        in1=mem.addends[:, TRI[qc]:TRI[qc] + n], scale=1.0, scalar=LOWEST,
                        op0=ALU.add, op1=ALU.max,
                        accum_out=mem.maxima[:, slot, g:g + 1]).then_inc(s.scores_read, 1)
                dve.wait_ge(s.scores_read, HPG * (i + 1))
                diag = mem.probs[:, slot, :, EXTRAS + qc * P:EXTRAS + n]
                nc.vector.tensor_tensor(diag, diag, mem.replacing[:, qc, :].unsqueeze(1).to_broadcast([P, HPG, P]), ALU.max)
                dve.wait_ge(s.product_kept, place["image", hg] + 1)
                image = mem.image_scores[:, hg % 2, HPG * qc:HPG * (qc + 1)]
                nc.vector.tensor_copy(mem.probs[:, slot, :, 1], image)
                nc.vector.scalar_tensor_tensor(out=mem.top[:, :], in0=mem.maxima[:, slot, :],
                                               scalar=mem.masked_max[:, 0:1], in1=image,
                                               op0=ALU.max, op1=ALU.max).then_inc(s.top, 1)
                dve.wait_ge(s.top, i + 1)
                nc.vector.tensor_scalar(mem.neg_max[:, slot, :], mem.top[:, :], -1.0, None,
                                        ALU.mult).then_inc(s.maxima_ready, 1)

            def normalise(i):
                slot = i % RING
                dve.wait_ge(s.exps_done, HPG * (i + 1))
                qc = units[i][1]
                nc.vector.scalar_tensor_tensor(out=mem.sums[:, slot, :], in0=mem.probs[:, slot, :, 0],
                                               scalar=mem.tail_sum[:, qc:qc + 1], in1=mem.sums[:, slot, :],
                                               op0=ALU.mult, op1=ALU.add).then_inc(s.scales, 1)
                dve.wait_ge(s.scales, 2 * i + 1)
                nc.vector.reciprocal(mem.scales[:, slot, :], mem.sums[:, slot, :]).then_inc(s.scales, 1)
                dve.wait_ge(s.scales, 2 * i + 2)
                nc.vector.tensor_tensor(mem.extras[:, slot, :].rearrange("p (g e) -> p g e", e=EXTRAS),
                                        mem.probs[:, slot, :, 0:EXTRAS],
                                        mem.scales[:, slot, :].unsqueeze(2).to_broadcast([P, HPG, EXTRAS]), ALU.mult)
                for g in range(HPG):
                    row = mem.probs[:, slot, g, EXTRAS:EXTRAS + P * (qc + 1)]
                    nc.vector.tensor_scalar(row, row, mem.scales[:, slot, g:g + 1], None,
                                            ALU.mult).then_inc(s.probs_ready, 1)

            dve.wait_ge(s.rows_made, 1)
            nc.vector.tensor_copy(mem.mask_all[:, :], mem.banks[7][:, :]).then_inc(s.mask_made, 1)
            nc.vector.tensor_scalar(mem.masked_all[:, :], mem.banks[7][:, :], MASK_OUT, None,
                                    ALU.add).then_inc(s.mask_made, 1)
            nc.vector.tensor_scalar(mem.masked_col[:, :], mem.banks[4][:, 0:QC], MASK_OUT, None, ALU.add)
            dve.wait_ge(s.mask_made, 2)
            nc.vector.tensor_reduce(mem.masked_max[:, :], mem.masked_all[:, :], AX.X, ALU.max).then_inc(s.mask_made, 1)
            for job in at_start[:2]:
                keep(*job)
            dve.wait_ge(s.mask_made, 3)
            nc.vector.tensor_scalar(mem.neg_masked[:, :], mem.masked_max[:, :], -1.0, None,
                                    ALU.mult).then_inc(s.masked_ready, 1)
            for qc in range(QC):
                at, n = TRI[qc], P * qc
                if qc:
                    nc.vector.tensor_copy(mem.addends[:, at:at + n], mem.mask_all[:, 0:n])
                nc.vector.tensor_tensor(mem.addends[:, at + n:at + n + P], mem.mask_all[:, n:n + P],
                                        mem.drop_masked[:, :], ALU.add)
                ins = nc.vector.tensor_tensor(mem.replacing[:, qc, :], mem.masked_all[:, n:n + P],
                                              mem.drop_kept[:, :], ALU.add)
            ins.then_inc(s.addends_ready, 1)
            keep(*at_start[2])
            dve.wait_ge(s.image_made, 1)
            nc.vector.tensor_copy(mem.v_extra[:, :, :], mem.banks[5][:, :].rearrange("p (h c) -> p h c", h=HG)).then_inc(s.image_kept, 1)
            nc.vector.tensor_copy(mem.xT[:, :, :], mem.X[:, :, bass.ds(b, 1), :].rearrange("p k o t -> p k (o t)")).then_inc(s.x_in_place, 1)
            dve.wait_ge(s.addends_ready, 1)
            dve.wait_ge(s.hidden_exp, 1)
            dve.wait_ge(s.image_b, 2)
            for kc in range(1, QC):
                dst = mem.hidden_w[:, kc - 1, :].rearrange("p (q g e) -> p q g e", q=QC, e=EXTRAS)[:, 0:kc, 0:HPG, 0]
                nc.vector.tensor_copy(dst, mem.hidden_col[:, kc:kc + 1].unsqueeze(2).to_broadcast([P, kc, HPG]))
            dve.wait_ge(s.image_kept, 1)
            for i in range(UNITS + LAG + 2):
                if i < UNITS:
                    for job in ahead[i]:
                        keep(*job)
                    scores_of(i)
                if 1 <= i <= UNITS:
                    normalise(i - 1)
                if i < UNITS:
                    for job in at_step[i]:
                        keep(*job)
                hg = group_ended(i - 1) if i else None
                if hg is not None:
                    dve.wait_ge(s.weighed, hg + 1)
                    nc.vector.tensor_copy(mem.attnT[:, hg, :], mem.banks[7][:, :]).then_inc(s.weighed_kept, 1)
            for tc in range(QC):
                dve.wait_ge(s.projected, tc + 1)
                if tc >= 2:
                    dve.wait_ge(s.out_sent[tc % 2], 16)
                nc.vector.tensor_tensor(mem.out_rows[:, tc % 2, :], mem.banks[tc][:, :],
                                        mem.bias_tiles[:, 1, :], ALU.add).then_inc(s.out_rows, 1)

        @block.gpsimd
        def _(pool):
            nc.gpsimd.tensor_copy(mem.k_image_b[:, :, :], mem.k_image[:, bass.ds(b, 1), :, :].rearrange("p o h g -> p (o h) g")).then_inc(s.image_b, 1)
            nc.gpsimd.memset(mem.widened[:, :, :], 0.0).then_inc(s.wide_zero, 1)
            pool.wait_ge(s.wide_zero, 1)
            nc.gpsimd.tensor_copy(
                mem.v_image_wide[:, :, :].rearrange("p h (q g e) -> p h q g e", q=QC, e=EXTRAS)[:, :, :, 0:HPG, 1],
                mem.v_image[:, bass.ds(b, 1), :, :].rearrange("p o h g -> p (o h) g").unsqueeze(2).to_broadcast([P, HG, QC, HPG])).then_inc(s.image_b, 1)

            def queries_alone(i):
                hg, qc = units[i]
                pool.wait_ge(s.product_kept, place["q", hg] + 1)
                if i >= 2:
                    pool.wait_ge(s.scores_done, HPG * (i - 1))
                nc.gpsimd.tensor_tensor(mem.q_alone[:, i % 2, :, :],
                                        mem.qT[:, qc * P:(qc + 1) * P].unsqueeze(1).to_broadcast([P, HPG, P]),
                                        mem.head_rows[:, :].unsqueeze(2).to_broadcast([P, HPG, P]),
                                        ALU.mult).then_inc(s.queries_alone, 1)

            for i in range(UNITS):
                queries_alone(i)


class Signals:

    def __init__(self, sem):
        self.all = []

        def new(name):
            self.all.append(sem(name))
            return self.all[-1]

        self.small_in = new("small_in")
        self.weights_in = new("weights_in")
        self.small_turned = new("small_turned")
        self.small_kept = new("small_kept")
        self.bias_kept = new("bias_kept")
        self.zeroed = new("zeroed")
        self.ident = new("ident")
        self.x_turned = new("x_turned")
        self.x_kept0 = new("x_kept0")
        self.x_kept1 = new("x_kept1")
        self.h0_new = new("h0_new")
        self.h12_new = new("h12_new")
        self.main0_done = new("main0_done")
        self.main12_done = new("main12_done")
        self.rows0_copied = new("rows0_copied")
        self.rows12_copied = new("rows12_copied")
        self.turned0 = new("turned0")
        self.turned12 = new("turned12")
        self.pre0 = new("pre0")
        self.pre12 = new("pre12")
        self.gates0 = new("gates0")
        self.gated0 = new("gated0")
        self.memory0 = new("memory0")
        self.tanh0 = new("tanh0")
        self.blend0 = new("blend0")
        self.fresh0 = new("fresh0")
        self.fill_done = new("fill_done")
        self.fill_kept = new("fill_kept")
        self.chunk_op = new("chunk_op")
        self.image_in = new("image_in")
        self.rows_made = new("rows_made")
        self.turned = new("turned")
        self.turn_kept = new("turn_kept")
        self.image_made = new("image_made")
        self.image_zero = new("image_zero")
        self.image_b = new("image_b")
        self.image_kept = new("image_kept")
        self.queries_alone = new("queries_alone")
        self.head_zero = new("head_zero")
        self.x_in_place = new("x_in_place")
        self.mask_made = new("mask_made")
        self.addends_ready = new("addends_ready")
        self.product_done = new("product_done")
        self.product_kept = new("product_kept")
        self.scores_done = new("scores_done")
        self.scores_read = new("scores_read")
        self.top = new("top")
        self.head_wide = new("head_wide")
        self.head_turned = new("head_turned")
        self.hidden_v = new("hidden_v")
        self.masked_ready = new("masked_ready")
        self.hidden_exp = new("hidden_exp")
        self.wide_zero = new("wide_zero")
        self.maxima_ready = new("maxima_ready")
        self.exps_done = new("exps_done")
        self.scales = new("scales")
        self.probs_ready = new("probs_ready")
        self.weighed = new("weighed")
        self.weighed_kept = new("weighed_kept")
        self.projected = new("projected")
        self.out_rows = new("out_rows")
        self.x_in = [new(f"x_in{q}") for q in range(4)]
        self.out_sent = [new(f"out_sent{q}") for q in range(2)]


def build(nc, a, out):
    mem = Mem()
    with ExitStack() as ctx:
        def sb(stack, name, shape):
            return stack.enter_context(nc.sbuf_tensor(name, shape, F32))

        def bank(name):
            return ctx.enter_context(nc.psum_tensor(name, [P, 512], F32))

        sems = Signals(lambda name: ctx.enter_context(nc.semaphore(name)))
        nums = [x.num for x in sems.all]
        assert nums == list(range(nums[0], nums[0] + len(nums)))
        mem.sem_range = range(nums[0], nums[-1] + 1)

        banks = [bank(f"bank{q}") for q in range(8)]
        mem.ps0, mem.ps12, mem.tp0, mem.tp12 = banks[0:4]
        mem.fillps = banks[4:6]
        mem.xps = banks[6:8]

        mem.X = sb(ctx, "X", [P, KC, B, T])
        mem.ident = sb(ctx, "ident", [P, P])
        mem.biasT = sb(ctx, "biasT", [P, NBIAS])
        mem.condT = sb(ctx, "condT", [P, KC, B])
        mem.banks = banks

        with ExitStack() as scan:
            mem.h0 = sb(scan, "h0", [P, SLOTS, KC, CH, B])
            mem.h12 = sb(scan, "h12", [P, SLOTS, 2, KC, CH, B])
            mem.wh0 = sb(scan, "wh0", [P, KC, KC, G0 // KC * P])
            mem.wx = [sb(scan, "wx0", [P, KC, 3 * D]), sb(scan, "wx1", [P, KC, D]), sb(scan, "wx2", [P, KC, D])]
            mem.wh12 = sb(scan, "wh12", [P, 2, KC, D])
            mem.xw0 = sb(scan, "xw0", [P, SLOTS, XW, CH, B])
            mem.xw12 = sb(scan, "xw12", [P, SLOTS, 2, KC, CH, B])
            mem.stage = [sb(scan, f"stage{l}", [P, KC, N]) for l in range(3)]
            mem.rows0 = sb(scan, "rows0", [P, G0 // KC * P])
            mem.rows12 = sb(scan, "rows12", [P, 2 * P])
            mem.pre0 = sb(scan, "pre0_sb", [P, G0, B])
            mem.gates0 = sb(scan, "gates0_sb", [P, 2 * KC, B])
            mem.gated0 = sb(scan, "gated0_sb", [P, KC, B])
            mem.mem0 = sb(scan, "mem0", [P, KC, B])
            mem.tanh0 = sb(scan, "tanh0_sb", [P, KC, B])
            mem.keep0 = sb(scan, "keep0", [P, KC, B])
            mem.held0 = sb(scan, "held0", [P, KC, B])
            mem.fresh0 = sb(scan, "fresh0_sb", [P, KC, B])
            mem.sum12 = sb(scan, "sum12", [P, 2, 4, B])
            with ExitStack() as load:
                mem.xrows = sb(load, "xrows", [P, 4, D])
                mem.bias_rows = sb(load, "bias_rows", [P, P])
                mem.cond_rows = sb(load, "cond_rows", [P, D])
                setup(nc, mem, sems, a)
                clear_signals(nc, mem)
            m = 0
            while m < ROUNDS:
                times = (NCH - 2 - m) // 2 if m == 6 else 1
                scan_rounds(nc, mem, sems, m, times)
                m += 2 * times
            add_last_chunk(nc, mem)
            clear_signals(nc, mem)

        mem.w_qkv = sb(ctx, "w_qkv", [P, KC, 3 * D])
        mem.w_proj = sb(ctx, "w_proj", [P, KC, D])
        mem.bias_tiles = sb(ctx, "bias_tiles", [P, 2, D])
        mem.drop_masked = sb(ctx, "drop_masked", [P, P])
        mem.drop_kept = sb(ctx, "drop_kept", [P, P])
        mem.ones = sb(ctx, "ones", [P, P])
        mem.k_image = sb(ctx, "k_image", [P, B, HG, HPG])
        mem.v_image = sb(ctx, "v_image", [P, B, HG, HPG])
        mem.head_rows = sb(ctx, "head_rows", [P, HPG])
        mem.q_bias = sb(ctx, "q_bias", [P, HG])
        mem.probsT = sb(ctx, "probsT", [P, HPG, QC, T])
        mem.xT = sb(ctx, "xT", [P, KC, T])
        mem.row_biases = mem.xT[:, 0:2, :]
        mem.probs_extra = sb(ctx, "probs_extra", [P, T])
        mem.head_block = sb(ctx, "head_block", [P, P])
        mem.tail_sum = sb(ctx, "tail_sum", [P, QC])
        mem.head_wide = mem.xT[:, 2, 0:P]
        mem.q_alone = sb(ctx, "q_alone", [P, 2, HPG, P])
        attention_setup(nc, mem, sems, a)
        clear_signals(nc, mem)
        mem.qT = sb(ctx, "qT", [P, T])
        mem.kT = sb(ctx, "kT", [P, 2, T])
        mem.v = sb(ctx, "v", [P, QC, D])
        mem.attnT = sb(ctx, "attnT", [P, HG, T])
        mem.probs = sb(ctx, "probs", [P, RING, HPG, EXTRAS + T])
        mem.extras = sb(ctx, "extras", [P, RING, HPG * EXTRAS])
        mem.mask_row = mem.qT
        mem.mask_all = mem.v[:, 0, :]
        mem.widened = mem.attnT[:, 0:2, :]
        mem.v_image_wide = mem.attnT[:, 0, :].rearrange("p (h c) -> p h c", h=HG)
        mem.hidden_w = mem.attnT[:, 1, 0:(QC - 1) * P].rearrange("p (k c) -> p k c", k=QC - 1)
        mem.hidden_rows = mem.probs[:, RING - 1, :, :]
        mem.masked_all = mem.attnT[:, 3, :]
        mem.hidden_v = mem.attnT[:, 3, :]
        mem.masked_col = sb(ctx, "masked_col", [P, QC])
        mem.hidden_col = sb(ctx, "hidden_col", [P, QC])
        mem.neg_masked = sb(ctx, "neg_masked", [P, 1])
        mem.masked_max = sb(ctx, "masked_max", [P, 1])
        mem.addends = sb(ctx, "addends", [P, TRI[-1]])
        mem.replacing = sb(ctx, "replacing", [P, QC, P])
        mem.image_scores = sb(ctx, "image_scores", [P, 2, HPG * QC])
        mem.k_image_b = sb(ctx, "k_image_b", [P, HG, HPG])
        mem.v_extra = sb(ctx, "v_extra", [P, HG, P])
        mem.maxima = sb(ctx, "maxima", [P, RING, HPG])
        mem.top = sb(ctx, "top_sb", [P, HPG])
        mem.neg_max = sb(ctx, "neg_max", [P, RING, HPG])
        mem.sums = sb(ctx, "sums", [P, RING, HPG])
        mem.scales = sb(ctx, "scales_sb", [P, RING, HPG])
        mem.out_rows = mem.probs[:, 0:1, 0:2, 0:T].rearrange("p r g t -> p (r g) t")
        with nc.Fori(0, B) as b:
            attention_batch(nc, mem, sems, a, out, b)
            clear_signals(nc, mem)


_INPUTS = {"x": "x", "cond": "cond_1024", "mask": "mask_Bx1x1xS_ff0",
           "w_W": "L0_cond_w_W", "w_b": "L0_cond_w_b", "wx_W": "L0_cond_wx_W", "wx_b": "L0_cond_wx_b",
           "wh_W": "L0_cond_wh_W", "wh_b": "L0_cond_wh_b", "L1_Wx": "L1_cond_Wx", "L1_Wh": "L1_cond_Wh",
           "L1_b": "L1_cond_b", "L2_Wx": "L2_cond_Wx", "L2_Wh": "L2_cond_Wh", "L2_b": "L2_cond_b",
           "qkv_w": "L3_cond_c_attn_w", "qkv_b": "L3_cond_c_attn_b", "proj_w": "L3_cond_c_proj_w",
           "proj_b": "L3_cond_c_proj_b", "uk_w": "L3_cond_uk_w", "uk_b": "L3_cond_uk_b",
           "uv_w": "L3_cond_uv_w", "uv_b": "L3_cond_uv_b"}


def kernel(**inputs):
    import numpy as _np
    import concourse.bacc as _bacc
    from concourse import mybir as _mybir
    from concourse.bass_utils import run_bass_kernel_spmd as _run

    nc = _bacc.Bacc("TRN2", target_bir_lowering=False, num_devices=1)
    arrays, args = {}, {}
    for short, name in _INPUTS.items():
        v = _np.ascontiguousarray(inputs[name])
        arrays[f"in_{name}_dram"] = v
        args[short] = nc.dram_tensor(f"in_{name}_dram", v.shape, _mybir.dt.from_np(v.dtype), kind="ExternalInput").ap()
    args["mask"] = args["mask"].rearrange("b o1 o2 t -> (b o1 o2) t")
    out = nc.dram_tensor("out_0_dram", (8, 512, 512), _mybir.dt.float32, kind="ExternalOutput").ap()
    build(nc, args, out)
    r = _run(nc, [arrays], core_ids=[0])
    return r.results[0]["out_0_dram"]
```

```python
from contextlib import ExitStack

import concourse.bass as bass
from concourse import mybir

F32 = mybir.dt.float32
ALU = mybir.AluOpType
ACT = mybir.ActivationFunctionType
AX = mybir.AxisListType

P = 128
B, T, D = 8, 512, 512
KC = D // P
CH = 16
NCH = T // CH
N = CH * B
ROUNDS = NCH + 4
G0 = 3 * KC
XW = G0 + KC
SLOTS = 2
PER_BLOCK = 4
RAMP = 8

BIAS_ROWS = [("w_b", 8), ("wh_b", 4), ("wx_b", 4), ("b1", 4), ("b2", 4),
             ("qkv_b", 12), ("proj_b", 4), ("uk_b", 4), ("uv_b", 4)]
BIAS_AT = {}
_at = 0
for _name, _n in BIAS_ROWS:
    BIAS_AT[_name] = _at
    _at += _n
NBIAS = _at


def fills_of(m):
    out = []
    if -1 <= m < NCH - 1:
        out += [(0, g) for g in range(G0)]
    if 0 <= m - 1 < NCH:
        out += [(1, g) for g in range(KC)]
    if 0 <= m - 3 < NCH:
        out += [(2, g) for g in range(KC)]
    return out


def plan(m):
    fills = fills_of(m)
    n = len(fills)
    late = 0 if m < NCH - 1 else 3
    by_step = [[]] * late + [fills[n * s // (CH - late):n * (s + 1) // (CH - late)] for s in range(CH - late)]
    chunk_ops = [[] for _ in range(CH)]
    if m < NCH - 1:
        chunk_ops[0].append(("stage", 0, m + 1))
    at = 1
    for layer, c in ((1, m - 1), (2, m - 3)):
        if 0 <= c < NCH:
            chunk_ops[at].append(("add", layer - 1, c))
            chunk_ops[at + 1].append(("stage", layer, c))
        at += 2
    if 0 <= m - 5 < NCH:
        chunk_ops[at].append(("add", 2, m - 5))
    layers = [l for l, c in ((0, m - 2), (1, m - 4)) if 0 <= c < NCH]
    return {"scan0": 0 <= m < NCH, "scan12": layers, "fills": by_step, "chunk_ops": chunk_ops}


class Mem:
    pass


def clear_signals(nc, mem):
    nc.all_engine_barrier(sems_to_clear=mem.sem_range)


def scan_rounds(nc, mem, sems, a, first, times):
    plans = [plan(first + u) for u in range(PER_BLOCK)]
    steps = [(u, t) for u in range(PER_BLOCK) for t in range(CH)]
    S = len(steps)
    if times > 1:
        with nc.Fori(0, times) as i:
            scan_block(nc, mem, sems, a, plans, steps, S, first, i)
            clear_signals(nc, mem)
    else:
        scan_block(nc, mem, sems, a, plans, steps, S, first, None)
        clear_signals(nc, mem)


def scan_block(nc, mem, sems, a, plans, steps, S, first, i):
    s = sems
    X, stage, h0, h12, xw0, xw12 = mem.X, mem.stage, mem.h0, mem.h12, mem.xw0, mem.xw12

    def counts(per_step):
        out = [0]
        for u, t in steps:
            out.append(out[-1] + per_step(u, t))
        return out

    n0 = counts(lambda u, t: int(plans[u]["scan0"]))
    n12 = counts(lambda u, t: int(bool(plans[u]["scan12"])))
    nfill = counts(lambda u, t: len(plans[u]["fills"][t]))
    nchunk = counts(lambda u, t: len(plans[u]["chunk_ops"][t]))
    staged = {}
    q = 0
    for u, t in steps:
        for kind, layer, c in plans[u]["chunk_ops"][t]:
            q += 1
            if kind == "stage":
                staged[u, layer] = q
    last_fill = {}
    q = 0
    for u, t in steps:
        for layer, g in plans[u]["fills"][t]:
            q += 1
            last_fill[u, layer] = q

    def before(u, t):
        return (u % 2, t - 1) if t else (1 - u % 2, CH - 1)

    with nc.Block(no_gpsimd_drain=True) as block:

        if first == 0:
            @block.sync
            def _(sp):
                for l in (1, 2):
                    for dst, src in ((mem.wx[l], a[f"L{l}_Wx"]), (mem.wh12[:, l - 1, :, :], a[f"L{l}_Wh"])):
                        sp.dma_start(dst[:, :, :], src.rearrange("(k p) n -> p k n", p=P)).then_inc(s.weights_in, 16)
                sp.wait_ge(s.weights_in, 64)

        if first >= NCH:
            @block.sync
            def _(sp):
                loads = [(mem.uk_rows, a["uk_w"]), (mem.uv_rows, a["uv_w"]), (mem.w_proj, a["proj_w"]),
                         (mem.w_qkv, a["qkv_w"])]
                for dst, src in loads:
                    sp.dma_start(dst[:, :, :], src.rearrange("(k p) n -> p k n", p=P)).then_inc(s.weights_in, 16)
                sp.wait_ge(s.weights_in, 16 * len(loads))

        @block.tensor
        def _(pe):
            def main0(n, u, t):
                if n0[n]:
                    pe.wait_ge(s.h0_new, n0[n])
                us, ts = before(u, t)
                for k in range(KC):
                    for j in range(KC):
                        mm = pe.matmul(mem.ps0[32 * j:32 * j + B, 0:G0 // KC * P],
                                       h0[:, us, k, ts, :], mem.wh0[:, k, j, :],
                                       start=(k == 0), stop=(k == KC - 1))
                mm.then_inc(s.main0_done, 1)

            def main12(n, u, t, ks):
                if n12[n] and ks[0] == 0:
                    pe.wait_ge(s.h12_new, n12[n])
                us, ts = before(u, t)
                for k in ks:
                    for l in plans[u]["scan12"]:
                        for j in range(2):
                            at = 32 * (2 * l + j)
                            mm = pe.matmul(mem.ps12[at:at + B, 0:2 * P],
                                           h12[:, us, l, k, ts, :],
                                           mem.wh12[:, l, k, 2 * P * j:2 * P * (j + 1)],
                                           start=(k == 0), stop=(k == KC - 1))
                if ks[-1] == KC - 1:
                    mm.then_inc(s.main12_done, 1)

            for n, (u, t) in enumerate(steps):
                p = plans[u]
                if p["scan0"]:
                    main0(n, u, t)
                if p["scan12"]:
                    main12(n, u, t, (0, 1))
                if p["scan0"]:
                    pe.wait_ge(s.rows0_copied, n0[n] + 1)
                    for g in range(G0 // KC):
                        mm = pe.transpose(mem.tp0[:, g * P:(g + 1) * P],
                                          mem.rows0[:, g * P:(g + 1) * P], mem.ident[:, :])
                    mm.then_inc(s.turned0, 1)
                if p["scan12"]:
                    main12(n, u, t, (2, 3))
                if n >= 2 and p["fills"][t] and nfill[n - 1]:
                    pe.wait_ge(s.fill_kept, nfill[n - 1])
                for f, (layer, g) in enumerate(p["fills"][t]):
                    pe.wait_ge(s.chunk_op, staged[u, layer])
                    if first == 0 and layer:
                        pe.wait_ge(s.weights_in, 64)
                    w = mem.wx[layer]
                    for k in range(KC):
                        mm = pe.matmul(mem.fillps[n % 2][:, f * N:(f + 1) * N], w[:, k, g * P:(g + 1) * P],
                                       stage[layer][:, k, :], start=(k == 0), stop=(k == KC - 1))
                    mm.then_inc(s.fill_done, 1)
                if p["scan12"]:
                    pe.wait_ge(s.rows12_copied, n12[n] + 1)
                    for g in range(2):
                        mm = pe.transpose(mem.tp12[:, g * P:(g + 1) * P],
                                          mem.rows12[:, g * P:(g + 1) * P], mem.ident[:, :])
                    mm.then_inc(s.turned12, 1)

        @block.scalar
        def _(act):
            def tanh12(n, u, t):
                act.wait_ge(s.pre12, n12[n] + 1)
                ls = plans[u]["scan12"]
                l0, l1 = 2 * ls[0], 2 * ls[-1] + 2
                nc.scalar.activation(
                    h12[:, u % 2, :, :, t, :].rearrange("p l (j g) b -> p g (l j) b", g=2)[:, :, l0:l1, :],
                    mem.sum12[:, :, l0:l1, :], ACT.Tanh).then_inc(s.h12_new, 1)

            for n, (u, t) in enumerate(steps):
                p = plans[u]
                if n:
                    v, w = steps[n - 1]
                    if plans[v]["scan12"]:
                        tanh12(n - 1, v, w)
                if n and t == 0 and p["scan12"] and nchunk[n]:
                    act.wait_ge(s.chunk_op, nchunk[n])
                if p["scan0"]:
                    act.wait_ge(s.main0_done, n0[n] + 1)
                    nc.scalar.copy(mem.rows0[:, :], mem.ps0[:, 0:G0 // KC * P]).then_inc(s.rows0_copied, 1)
                    act.wait_ge(s.pre0, n0[n] + 1)
                    nc.scalar.activation(mem.gates0[:, :, :], mem.pre0[:, 0:2 * KC, :],
                                         ACT.Sigmoid).then_inc(s.gates0, 1)
                    act.wait_ge(s.memory0, n0[n] + 1)
                    nc.scalar.activation(mem.tanh0[:, :, :], mem.mem0[:, :, :],
                                         ACT.Tanh).then_inc(s.tanh0, 1)
                if p["scan12"]:
                    act.wait_ge(s.main12_done, n12[n] + 1)
                    nc.scalar.copy(mem.rows12[:, :], mem.ps12[:, 0:2 * P]).then_inc(s.rows12_copied, 1)
            u, t = steps[-1]
            if plans[u]["scan12"]:
                tanh12(S - 1, u, t)

        @block.vector
        def _(dve):
            def pre12(n, u, t):
                ls = plans[u]["scan12"]
                l0, l1 = 2 * ls[0], 2 * ls[-1] + 2
                dve.wait_ge(s.turned12, n12[n] + 1)
                nc.vector.tensor_tensor(
                    mem.sum12[:, :, l0:l1, :],
                    mem.tp12[:, 0:2 * P].rearrange("p (g j c) -> p g j c", g=2, j=4)[:, :, l0:l1, 0:B],
                    xw12[:, u % 2, :, :, t, :].rearrange("p l (j g) b -> p g (l j) b", g=2)[:, :, l0:l1, :],
                    ALU.add).then_inc(s.pre12, 1)

            def keep_fills(n, u, t):
                if plans[u]["fills"][t]:
                    dve.wait_ge(s.fill_done, nfill[n + 1])
                for f, (layer, g) in enumerate(plans[u]["fills"][t]):
                    if layer == 0:
                        at = g if g < 2 * KC else g + KC
                        dst = xw0[:, 1 - u % 2, at, :, :]
                        bias = BIAS_AT["w_b"] + g if g < 2 * KC else BIAS_AT["wx_b"] + g - 2 * KC
                    else:
                        dst = xw12[:, 1 - u % 2, layer - 1, g, :, :]
                        bias = BIAS_AT[f"b{layer}"] + g
                    nc.vector.tensor_scalar(
                        dst, mem.fillps[n % 2][:, f * N:(f + 1) * N].rearrange("p (t b) -> p t b", b=B),
                        mem.biasT[:, bias:bias + 1], None, ALU.add).then_inc(s.fill_kept, 1)

            for n, (u, t) in enumerate(steps):
                p = plans[u]
                if n:
                    v, w = steps[n - 1]
                    if plans[v]["scan12"]:
                        pre12(n - 1, v, w)
                    keep_fills(n - 1, v, w)
                if n and t == 0 and nfill[n]:
                    dve.wait_ge(s.fill_kept, nfill[n])
                if p["scan0"]:
                    dve.wait_ge(s.turned0, n0[n] + 1)
                    nc.vector.tensor_tensor(
                        mem.pre0[:, :, :],
                        mem.tp0[:, 0:G0 // KC * P].rearrange("p (g c) -> p g c", c=32)[:, :, 0:B],
                        xw0[:, u % 2, 0:G0, t, :], ALU.add).then_inc(s.pre0, 1)
                    dve.wait_ge(s.gates0, n0[n] + 1)
                    nc.vector.tensor_tensor(mem.gated0[:, :, :], mem.gates0[:, 0:KC, :],
                                            mem.pre0[:, 2 * KC:G0, :], ALU.mult).then_inc(s.gated0, 1)
                    dve.wait_ge(s.gated0, n0[n] + 1)
                    nc.vector.tensor_tensor(mem.mem0[:, :, :], mem.gated0[:, :, :],
                                            xw0[:, u % 2, G0:XW, t, :], ALU.add).then_inc(s.memory0, 1)
                    dve.wait_ge(s.tanh0, n0[n] + 1)
                    dve.wait_ge(s.blend0, 2 * n0[n] + 2)
                    nc.vector.tensor_tensor(mem.fresh0[:, :, :], mem.keep0[:, :, :],
                                            mem.tanh0[:, :, :], ALU.mult).then_inc(s.fresh0, 1)
                    dve.wait_ge(s.fresh0, n0[n] + 1)
                    nc.vector.tensor_tensor(h0[:, u % 2, :, t, :], mem.fresh0[:, :, :],
                                            mem.held0[:, :, :], ALU.add).then_inc(s.h0_new, 1)
            u, t = steps[-1]
            if plans[u]["scan12"]:
                pre12(S - 1, u, t)
            keep_fills(S - 1, u, t)

        @block.gpsimd
        def _(pool):
            def x_chunk(c):
                if i is None:
                    return X[:, :, :, c * CH:(c + 1) * CH]
                return X[:, :, :, bass.ds(i * (PER_BLOCK * CH) + c * CH, CH)]

            done = 0
            for n, (u, t) in enumerate(steps):
                p = plans[u]
                for kind, layer, c in p["chunk_ops"][t]:
                    if kind == "stage":
                        if done:
                            pool.wait_ge(s.chunk_op, done)
                        if u and (u - 1, layer) in last_fill:
                            pool.wait_ge(s.fill_done, last_fill[u - 1, layer])
                        nc.gpsimd.tensor_copy(
                            stage[layer][:, :, :].rearrange("p k (t b) -> p k b t", b=B),
                            x_chunk(c)).then_inc(s.chunk_op, 1)
                    else:
                        if u:
                            if layer == 0:
                                pool.wait_ge(s.h0_new, n0[CH * u])
                            else:
                                pool.wait_ge(s.h12_new, n12[CH * u])
                        ring = h0[:, 1 - u % 2, :, :, :] if layer == 0 else h12[:, 1 - u % 2, layer - 1, :, :, :]
                        nc.gpsimd.tensor_tensor(x_chunk(c), x_chunk(c),
                                                ring.rearrange("p k t b -> p k b t"),
                                                ALU.add).then_inc(s.chunk_op, 1)
                    done += 1
                if p["scan0"]:
                    us, ts = before(u, t)
                    if n0[n]:
                        pool.wait_ge(s.h0_new, n0[n])
                    pool.wait_ge(s.gates0, n0[n] + 1)
                    nc.gpsimd.tensor_scalar(mem.keep0[:, :, :], mem.gates0[:, KC:2 * KC, :],
                                            -1.0, 1.0, ALU.mult, ALU.add).then_inc(s.blend0, 1)
                    nc.gpsimd.tensor_tensor(mem.held0[:, :, :], mem.gates0[:, KC:2 * KC, :],
                                            h0[:, us, :, ts, :], ALU.mult).then_inc(s.blend0, 1)


def add_last_chunk(nc, mem):
    with nc.Block(no_gpsimd_drain=True) as block:

        @block.gpsimd
        def _(pool):
            last = mem.X[:, :, :, T - CH:T]
            nc.gpsimd.tensor_tensor(last, last,
                                    mem.h12[:, (NCH - 1) % 2, 1, :, :, :].rearrange("p k t b -> p k b t"), ALU.add)


def setup(nc, mem, sems, a):
    s = sems
    NT = T // P
    tiles = [(b, tc) for b in range(B) for tc in range(NT)]
    loads = []
    for k in range(KC):
        rows = slice(k * P, (k + 1) * P)
        hrows = slice(D + k * P, D + (k + 1) * P)
        for g, src in enumerate((a["w_W"][hrows, 0:D], a["w_W"][hrows, D:2 * D], a["wh_W"][rows, :])):
            loads.append((mem.wh0[:, k, :, g * P:(g + 1) * P], src.rearrange("p (j c) -> p j c", c=P)))
        loads.append((mem.wx[0][:, k, 0:2 * D], a["w_W"][rows, :]))
        loads.append((mem.wx[0][:, k, 2 * D:3 * D], a["wx_W"][rows, :]))
    names = {"w_b": "w_b", "wh_b": "wh_b", "wx_b": "wx_b", "b1": "L1_b", "b2": "L2_b",
             "qkv_b": "qkv_b", "proj_b": "proj_b", "uk_b": "uk_b", "uv_b": "uv_b"}
    XR = 4

    with nc.Block(no_gpsimd_drain=True) as block:

        @block.sync
        def _(sp):
            sp.dma_start(mem.cond_rows[0:B, :], a["cond"]).then_inc(s.small_in, 16)
            for name, n in BIAS_ROWS:
                at = BIAS_AT[name]
                sp.dma_start(mem.bias_rows[at:at + n, :],
                             a[names[name]].rearrange("(r c) -> r c", c=P)).then_inc(s.small_in, 16)
            for q, (b, tc) in enumerate(tiles):
                if q >= XR:
                    sp.wait_ge(s.x_turned, q - XR + 1)
                sp.dma_start(mem.xrows[:, q % XR, :],
                             a["x"][b, tc * P:(tc + 1) * P, :]).then_inc(s.x_in[q % XR], 16)

        @block.scalar
        def _(act):
            for dst, src in loads:
                act.dma_start(dst, src).then_inc(s.weights_in, 16)
            for q, (b, tc) in enumerate(tiles):
                if q % 2:
                    act.wait_ge(s.x_turned, q + 1)
                    nc.scalar.copy(mem.X[:, :, b, tc * P:(tc + 1) * P],
                                   mem.xps[q % 2][:, :].rearrange("p (k t) -> p k t", k=KC)).then_inc(s.x_kept1, 1)
            act.wait_ge(s.weights_in, 16 * len(loads))

        @block.gpsimd
        def _(pool):
            nc.gpsimd.memset(mem.ident[:, :], 0.0).then_inc(s.ident, 1)
            pool.wait_ge(s.ident, 1)
            nc.gpsimd.affine_select(out=mem.ident[:, :], in_=mem.ident[:, :], compare_op=ALU.not_equal,
                                    fill=1.0, base=0, pattern=[[-1, P]],
                                    channel_multiplier=1).then_inc(s.ident, 1)
            nc.gpsimd.memset(mem.xw0[:, :, G0 - KC:G0, :, :], 0.0).then_inc(s.zeroed, 1)
            pool.wait_ge(s.x_kept0, len(tiles) // 2)
            pool.wait_ge(s.x_kept1, len(tiles) // 2)
            nc.gpsimd.tensor_copy(mem.stage[0][:, :, :].rearrange("p k (t b) -> p k b t", b=B),
                                  mem.X[:, :, :, 0:CH]).then_inc(s.chunk_op, 1)

        @block.tensor
        def _(pe):
            pe.wait_ge(s.ident, 2)
            pe.wait_ge(s.small_in, 16 * (1 + len(BIAS_ROWS)))
            for k in range(KC):
                pe.transpose(mem.fillps[0][:, B * k:B * (k + 1)],
                             mem.cond_rows[0:B, k * P:(k + 1) * P], mem.ident[0:B, 0:B])
            pe.transpose(mem.fillps[1][:, 0:NBIAS], mem.bias_rows[0:NBIAS, :],
                         mem.ident[0:NBIAS, 0:NBIAS]).then_inc(s.small_turned, 1)
            for q in range(len(tiles)):
                pe.wait_ge(s.x_in[q % XR], 16 * (q // XR + 1))
                if q >= 2:
                    pe.wait_ge(s.x_kept0 if q % 2 == 0 else s.x_kept1, q // 2)
                for k in range(KC):
                    mm = pe.transpose(mem.xps[q % 2][:, k * P:(k + 1) * P],
                                      mem.xrows[:, q % XR, k * P:(k + 1) * P], mem.ident[:, :])
                mm.then_inc(s.x_turned, 1)
            pe.wait_ge(s.weights_in, 16 * len(loads))
            pe.wait_ge(s.chunk_op, 1)
            pe.wait_ge(s.small_kept, 1)
            for f, (layer, g) in enumerate(fills_of(-1)):
                if f >= 2:
                    pe.wait_ge(s.fill_kept, f - 1)
                for k in range(KC):
                    mm = pe.matmul(mem.fillps[f % 2][:, 0:N], mem.wx[0][:, k, g * P:(g + 1) * P],
                                   mem.stage[0][:, k, :], start=(k == 0), stop=(k == KC - 1))
                mm.then_inc(s.fill_done, 1)

        @block.vector
        def _(dve):
            nc.vector.memset(mem.ps0[:, :], 0.0)
            nc.vector.memset(mem.ps12[:, :], 0.0)
            dve.wait_ge(s.small_turned, 1)
            nc.vector.tensor_copy(mem.biasT[:, :], mem.fillps[1][:, 0:NBIAS]).then_inc(s.bias_kept, 1)
            cond = mem.fillps[0][:, 0:B * KC].rearrange("p (k b) -> p k b", b=B)
            nc.vector.tensor_copy(mem.h0[:, 1, :, CH - 1, :], cond)
            nc.vector.tensor_copy(mem.h12[:, 1, 0, :, CH - 1, :], cond)
            nc.vector.tensor_copy(mem.h12[:, 1, 1, :, CH - 1, :], cond)
            nc.vector.tensor_copy(mem.condT[:, :, :], cond).then_inc(s.small_kept, 1)
            dve.wait_ge(s.bias_kept, 1)
            dve.wait_ge(s.zeroed, 1)
            for slot in range(SLOTS):
                for g in range(KC):
                    at = BIAS_AT["wh_b"] + g
                    addend = mem.xw0[:, slot, G0 - KC + g, :, :]
                    nc.vector.tensor_scalar(addend, addend, mem.biasT[:, at:at + 1], None, ALU.add)
            for q, (b, tc) in enumerate(tiles):
                if q % 2 == 0:
                    dve.wait_ge(s.x_turned, q + 1)
                    nc.vector.tensor_copy(mem.X[:, :, b, tc * P:(tc + 1) * P],
                                          mem.xps[q % 2][:, :].rearrange("p (k t) -> p k t", k=KC)).then_inc(s.x_kept0, 1)
            for f, (layer, g) in enumerate(fills_of(-1)):
                dve.wait_ge(s.fill_done, f + 1)
                at = g if g < 2 * KC else g + KC
                bias = BIAS_AT["w_b"] + g if g < 2 * KC else BIAS_AT["wx_b"] + g - 2 * KC
                nc.vector.tensor_scalar(mem.xw0[:, 0, at, :, :],
                                        mem.fillps[f % 2][:, 0:N].rearrange("p (t b) -> p t b", b=B),
                                        mem.biasT[:, bias:bias + 1], None, ALU.add).then_inc(s.fill_kept, 1)


BATCHES = 4
HG = 4
HPG = 4
HD = P // HPG
QC = T // P
UNITS = HG * QC
RING = 3
LAG = 2
PER_TURN = [4, 2, 1, 1]
TURNS = [HPG // n + 1 for n in PER_TURN]
EXTRAS = 2
FAR = 32
MASK_OUT = -10000.0
FAR_DOWN = -1.0e30
LOWEST = -3.0e38
TRI = [0, P, 3 * P, 6 * P, 10 * P]


def attention_setup(nc, mem, sems, a):
    s = sems
    uk_rows, uv_rows = mem.uk_rows, mem.uv_rows
    ukT, uvT = mem.probsT[:, 2, :, :], mem.probsT[:, 3, :, :]
    turns = [(rows, dst, o, k) for rows, dst in ((uk_rows, ukT), (uv_rows, uvT)) for k in range(KC) for o in range(KC)]
    NTURN = len(turns) // KC

    with nc.Block(no_gpsimd_drain=True) as block:

        @block.sync
        def _(sp):
            sp.dma_start(mem.row_biases[0:1, 0, :],
                         a["qkv_b"][2 * D:3 * D].rearrange("(o n) -> o n", o=1)).then_inc(s.small_in, 16)
            sp.dma_start(mem.row_biases[0:1, 1, :],
                         a["proj_b"].rearrange("(o n) -> o n", o=1)).then_inc(s.small_in, 16)

        @block.gpsimd
        def _(pool):
            nc.gpsimd.memset(mem.ones[:, :], 1.0).then_inc(s.ident, 1)
            nc.gpsimd.memset(mem.drop_masked[:, :], 0.0).then_inc(s.zeroed, 1)
            nc.gpsimd.memset(mem.drop_kept[:, :], LOWEST).then_inc(s.zeroed, 1)
            pool.wait_ge(s.zeroed, 2)
            nc.gpsimd.affine_select(out=mem.drop_masked[:, :], in_=mem.drop_masked[:, :],
                                    compare_op=ALU.is_ge, fill=FAR_DOWN, base=0,
                                    pattern=[[-1, P]], channel_multiplier=1).then_inc(s.zeroed, 1)
            nc.gpsimd.affine_select(out=mem.drop_kept[:, :], in_=mem.drop_kept[:, :],
                                    compare_op=ALU.is_ge, fill=0.0, base=0,
                                    pattern=[[-1, P]], channel_multiplier=1).then_inc(s.zeroed, 1)
            nc.gpsimd.memset(mem.probs_extra[:, :], 0.0)
            nc.gpsimd.memset(mem.head_wide[:, :], 0.0).then_inc(s.head_wide, 1)
            nc.gpsimd.memset(mem.k_image[:, :, :, :], 0.0).then_inc(s.image_zero, 1)
            nc.gpsimd.memset(mem.v_image[:, :, :, :], 0.0).then_inc(s.image_zero, 1)

        @block.tensor
        def _(pe):
            pe.wait_ge(s.ident, 1)
            pe.wait_ge(s.small_in, 32)
            for q in range(2):
                mm = pe.matmul(mem.banks[q][:, :], mem.ones[0:1, :], mem.row_biases[0:1, q, :],
                               start=True, stop=True)
            mm.then_inc(s.rows_made, 1)
            pe.wait_ge(s.head_wide, 2)
            pe.transpose(mem.banks[6][:, 0:P], mem.head_wide[:, :], mem.ident[:, :]).then_inc(s.head_turned, 1)
            for q in range(NTURN):
                if q >= 2:
                    pe.wait_ge(s.turn_kept, q - 1)
                for r in range(KC):
                    rows, dst, o, k = turns[q * KC + r]
                    mm = pe.transpose(mem.banks[2 + q % 2][:, o * P:(o + 1) * P],
                                      rows[:, o, k * P:(k + 1) * P], mem.ident[:, :])
                mm.then_inc(s.turned, 1)
            pe.wait_ge(s.turn_kept, NTURN)
            for q, wT in enumerate((ukT, uvT)):
                for o in range(KC):
                    for k in range(KC):
                        mm = pe.matmul(mem.banks[4 + q][:, B * o:B * (o + 1)],
                                       wT[:, k, o * P:(o + 1) * P], mem.condT[:, k, :],
                                       start=(k == 0), stop=(k == KC - 1))
            mm.then_inc(s.image_made, 1)

        @block.vector
        def _(dve):
            nc.vector.memset(mem.head_rows[:, :], 0.0).then_inc(s.head_zero, 1)
            dve.wait_ge(s.head_zero, 1)
            dve.wait_ge(s.head_wide, 1)
            for g in range(HPG):
                nc.vector.memset(mem.head_rows[HD * g:HD * (g + 1), g:g + 1], 1.0)
                ins = nc.vector.memset(mem.head_wide[HD * g:HD * (g + 1), :].rearrange("p (q c) -> p q c", q=QC)[:, :, EXTRAS * g], 1.0)
            ins.then_inc(s.head_wide, 1)
            nc.vector.memset(mem.tail_sum[:, :], 0.0)
            dve.wait_ge(s.head_turned, 1)
            nc.vector.tensor_copy(mem.head_block[:, :], mem.banks[6][:, 0:P])
            dve.wait_ge(s.rows_made, 1)
            for q in range(2):
                nc.vector.tensor_copy(mem.bias_tiles[:, q, :], mem.banks[q][:, :])
            for q in range(NTURN):
                dve.wait_ge(s.turned, q + 1)
                _, dst, _, k = turns[q * KC]
                nc.vector.tensor_copy(dst[:, k, :], mem.banks[2 + q % 2][:, :]).then_inc(s.turn_kept, 1)
            dve.wait_ge(s.image_made, 1)
            dve.wait_ge(s.image_zero, 2)
            for q, (dst, name) in enumerate(((mem.k_image, "uk_b"), (mem.v_image, "uv_b"))):
                for hg in range(HG):
                    for g in range(HPG):
                        rows = slice(HD * g, HD * (g + 1))
                        col = BIAS_AT[name] + hg
                        nc.vector.tensor_scalar(dst[rows, :, hg, g], mem.banks[4 + q][rows, B * hg:B * (hg + 1)],
                                                mem.biasT[rows, col:col + 1], None, ALU.add)
            at = BIAS_AT["qkv_b"]
            nc.vector.tensor_scalar(mem.q_bias[:, :], mem.biasT[:, at:at + HG], HD ** -0.5, None, ALU.mult)


def attention_batches(nc, mem, sems, a, out, part):
    s = sems
    units = [(hg, qc) for hg in range(HG) for qc in range(QC)]

    early = [("k", 0), ("q", 0)]
    at_start = [("v", 0), ("image", 0), ("v", 1), ("v", 2)]
    other_bank = {("v", 0): 1, ("image", 0): 2, ("v", 1): 3}
    at_step = {i: [] for i in range(UNITS)}
    for i, job in ((0, ("k", 1)), (1, ("q", 1)), (2, ("image", 1)), (3, ("v", 3)), (4, ("hidden", 0)),
                   (5, ("k", 2)), (6, ("q", 2)), (7, ("image", 2)), (8, ("k", 3)), (9, ("q", 3)),
                   (10, ("image", 3))):
        at_step[i].append(job)
    turned_by = [0]
    for _, qc in units:
        turned_by.append(turned_by[-1] + TURNS[qc])
    place = {}
    for job in early + at_start + [job for i in range(UNITS) for job in at_step[i]]:
        place[job] = len(place)
    PRODUCTS = len(place)
    HEADS = HPG * UNITS
    TURNED = turned_by[-1]

    def batch(u):
        return bass.ds(part * BATCHES + u, 1)

    def group_ended(i):
        v = i - LAG
        return units[v][0] if 0 <= v < UNITS and units[v][1] == QC - 1 else None

    with nc.Block(no_gpsimd_drain=True) as block:

        @block.sync
        def _(sp):
            for u in range(BATCHES):
                if u == 0:
                    sp.dma_start(mem.mask_row[0:1, :], a["mask"][batch(u), :]).then_inc(s.small_in, 16)
                if u + 1 < BATCHES:
                    sp.wait_ge(s.rows_made, u + 1)
                    sp.dma_start(mem.mask_row[0:1, :], a["mask"][batch(u + 1), :]).then_inc(s.small_in, 16)
                for tc in range(QC):
                    sp.wait_ge(s.out_rows, QC * u + tc + 1)
                    sp.dma_start(out[batch(u), tc * P:(tc + 1) * P, :].rearrange("o t n -> (o t) n"),
                                 mem.out_rows[:, tc % 2, :]).then_inc(s.out_sent[tc % 2], 16)
            sp.wait_ge(s.out_sent[0], 16 * QC // 2 * BATCHES)
            sp.wait_ge(s.out_sent[1], 16 * QC // 2 * BATCHES)

        @block.tensor
        def _(pe):
            def product(u, kind, c):
                n = place[kind, c]
                q = other_bank.get((kind, c), 6)
                bank = mem.banks[q]
                if q == 6:
                    before = n if (kind, c) != at_start[-1] else len(early)
                    if PRODUCTS * u + before:
                        pe.wait_ge(s.product_kept, PRODUCTS * u + before)
                elif u:
                    pe.wait_ge(s.out_rows, QC * (u - 1) + q + 1)
                if kind == "image":
                    pe.wait_ge(s.product_kept, PRODUCTS * u + place["q", c] + 1)
                    for qc in range(QC):
                        mm = pe.matmul(bank[:, HPG * qc:HPG * (qc + 1)],
                                       mem.qT[:, qc * P:(qc + 1) * P], mem.k_image_b[:, c, :],
                                       start=True, stop=True)
                elif kind == "hidden":
                    for kc in range(1, QC):
                        mm = pe.matmul(bank[:, :], mem.hidden_w[:, kc - 1, :], mem.v[:, kc, :],
                                       start=(kc == 1), stop=(kc == QC - 1))
                elif kind == "v":
                    for k in range(KC):
                        mm = pe.matmul(bank[:, :], mem.xT[:, k, c * P:(c + 1) * P],
                                       mem.w_qkv[:, k, 2 * D:3 * D], start=(k == 0), stop=(k == KC - 1))
                else:
                    at = (0 if kind == "q" else D) + c * P
                    for k in range(KC):
                        mm = pe.matmul(bank[:, :], mem.w_qkv[:, k, at:at + P],
                                       mem.X[:, k, batch(u), :].rearrange("p o t -> p (o t)"),
                                       start=(k == 0), stop=(k == KC - 1))
                mm.then_inc(s.product_done, 1)

            def scores(i):
                hg, qc = units[i]
                n = P * (qc + 1)
                pe.wait_ge(s.queries_alone, UNITS * u + i + 1)
                for g in range(HPG):
                    if i:
                        pe.wait_ge(s.scores_read, HEADS * u + HPG * (i - 1) + g + 1)
                    pe.matmul(mem.banks[g][:, 0:n], mem.q_alone[:, i % 2, g, :],
                              mem.kT[:, hg % 2, 0:n], start=True, stop=True).then_inc(s.scores_done, 1)

            def turn(v):
                qc = units[v][1]
                n, per = qc + 1, PER_TURN[qc]
                for r in range(TURNS[qc]):
                    q = turned_by[v] + r
                    if u or q >= 2:
                        pe.wait_ge(s.turn_kept, TURNED * u + q - 1)
                    bank = mem.banks[4 + q % 2]
                    if r < HPG // per:
                        for h in range(per):
                            g = per * r + h
                            pe.wait_ge(s.probs_ready, HEADS * u + HPG * v + g + 1)
                            for kc in range(n):
                                at = EXTRAS + kc * P
                                mm = pe.transpose(bank[:, (h * n + kc) * P:(h * n + kc + 1) * P],
                                                  mem.probs[:, v % RING, g, at:at + P], mem.ident[:, :])
                    else:
                        mm = pe.matmul(bank[FAR * qc:FAR * qc + EXTRAS * HPG, 0:P],
                                       mem.extras[:, v % RING, :], mem.ident[:, :], start=True, stop=True)
                    mm.then_inc(s.turned, 1)

            def weigh(hg):
                pe.wait_ge(s.turn_kept, TURNED * u + turned_by[QC * (hg + 1)])
                if hg == 0:
                    pe.wait_ge(s.product_kept, PRODUCTS * u + place["hidden", 0] + 1)
                else:
                    pe.wait_ge(s.weighed_kept, HG * u + hg)
                pe.matmul(mem.banks[7][:, :], mem.v_extra[:, hg, :], mem.probs_extra[:, :],
                          start=True, stop=False, skip_group_check=True)
                for kc in range(QC):
                    for g in range(HPG):
                        at = HD * (HPG * hg + g)
                        mm = pe.matmul(mem.banks[7][HD * g:HD * (g + 1), kc * P:T], mem.v[:, kc, at:at + HD],
                                       mem.probsT[:, g, kc, kc * P:T], start=False, stop=(kc == QC - 1),
                                       skip_group_check=True)
                mm.then_inc(s.weighed, 1)

            def project(tc):
                if tc == 0:
                    pe.wait_ge(s.weighed_kept, HG * u + HG - 1)
                pe.wait_ge(s.scores_read, HEADS * u + HPG * (UNITS - 1) + tc + 1)
                for k in range(HG - 1):
                    pe.matmul(mem.banks[tc][:, :], mem.attnT[:, k, tc * P:(tc + 1) * P],
                              mem.w_proj[:, k, :], start=(k == 0), stop=False, skip_group_check=True)
                for k in range(KC):
                    mm = pe.matmul(mem.banks[tc][:, k * P:(k + 1) * P], mem.xT[:, k, tc * P:(tc + 1) * P],
                                   mem.ident[:, :], start=False, stop=False, skip_group_check=True)
                return mm

            for job in early:
                product(0, *job)
            for u in range(BATCHES):
                pe.wait_ge(s.small_in, 16 * u + 16)
                pe.matmul(mem.banks[7][:, :], mem.ones[0:1, :], mem.mask_row[0:1, :],
                          start=True, stop=True)
                for kc in range(QC):
                    mm = pe.matmul(mem.banks[4][:, kc:kc + 1], mem.mask_row[0:1, kc * P:(kc + 1) * P],
                                   mem.ones[0:1, 0:1], start=True, stop=True)
                mm.then_inc(s.rows_made, 1)
                pe.wait_ge(s.x_in_place, u + 1)
                product(u, "v", 0)
                pe.wait_ge(s.image_b, 2 * u + 2)
                for hg in range(HG):
                    mm = pe.transpose(mem.banks[5][:, hg * P:(hg + 1) * P], mem.v_image_wide[:, hg, :], mem.ident[:, :])
                mm.then_inc(s.image_made, 1)
                for job in at_start[1:]:
                    product(u, *job)
                pe.wait_ge(s.addends_ready, u + 1)
                pe.wait_ge(s.image_kept, u + 1)
                pe.wait_ge(s.product_kept, PRODUCTS * u + place["v", 1] + 1)
                for i in range(UNITS + LAG + 1):
                    if i < UNITS:
                        scores(i)
                    if group_ended(i - 1) is not None:
                        weigh(group_ended(i - 1))
                    if i < UNITS:
                        for job in at_step[i]:
                            product(u, *job)
                    else:
                        if i < UNITS + len(early):
                            if u + 1 < BATCHES:
                                product(u + 1, *early[i - UNITS])
                            project(2 * (i - UNITS))
                            mm = project(2 * (i - UNITS) + 1)
                            mm.then_inc(s.projecting, 1)
                    if LAG <= i < UNITS + LAG:
                        turn(i - LAG)
                pe.wait_ge(s.weighed_kept, HG * u + HG)
                for tc in range(QC):
                    pe.matmul(mem.banks[tc][:, :], mem.attnT[:, HG - 1, tc * P:(tc + 1) * P],
                              mem.w_proj[:, HG - 1, :], start=False, stop=True,
                              skip_group_check=True).then_inc(s.projected, 1)

        @block.scalar
        def _(act):
            def exps(i):
                n = P * (units[i][1] + 1)
                act.wait_ge(s.maxima_ready, UNITS * u + i + 1)
                nc.scalar.activation(mem.probs[:, i % RING, :, 0], mem.neg_max[:, i % RING, :], ACT.Exp,
                                     bias=mem.masked_max[:, 0:1])
                for g in range(HPG):
                    row = mem.probs[:, i % RING, g, 1:EXTRAS + n]
                    nc.scalar.activation(row, row, ACT.Exp, bias=mem.neg_max[:, i % RING, g:g + 1],
                                         accum_out=mem.sums[:, i % RING, g:g + 1]).then_inc(s.exps_done, 1)

            def keep_turn(v):
                hg, qc = units[v]
                if qc == 0 and (u or hg):
                    act.wait_ge(s.weighed, HG * u + hg)
                n, per = qc + 1, PER_TURN[qc]
                for r in range(TURNS[qc]):
                    q = turned_by[v] + r
                    act.wait_ge(s.turned, TURNED * u + q + 1)
                    bank = mem.banks[4 + q % 2]
                    if r < HPG // per:
                        nc.scalar.copy(mem.probsT[:, per * r:per * (r + 1), 0:n, qc * P:(qc + 1) * P],
                                       bank[:, 0:per * n * P].rearrange("p (h k q) -> p h k q", h=per, k=n)).then_inc(s.turn_kept, 1)
                    else:
                        rows = slice(FAR * qc, FAR * qc + EXTRAS * HPG)
                        nc.scalar.copy(mem.probs_extra[rows, qc * P:(qc + 1) * P],
                                       bank[rows, 0:P]).then_inc(s.turn_kept, 1)

            for u in range(BATCHES):
                if u:
                    act.wait_ge(s.projecting, 2 * u)
                nc.scalar.copy(mem.xT[:, :, :], mem.X[:, :, batch(u), :].rearrange("p k o t -> p k (o t)")).then_inc(s.x_in_place, 1)
                act.wait_ge(s.masked_ready, u + 1)
                for qc in range(QC - 1):
                    nc.scalar.activation(mem.hidden_rows[:, qc, (qc + 1) * P:T], mem.masked_all[:, (qc + 1) * P:T], ACT.Exp,
                                         bias=mem.neg_masked[:, 0:1], accum_out=mem.tail_sum[:, qc:qc + 1])
                nc.scalar.activation(mem.hidden_col[:, :], mem.masked_col[:, :], ACT.Exp,
                                     bias=mem.neg_masked[:, 0:1]).then_inc(s.hidden_exp, 1)
                for i in range(UNITS + LAG):
                    if 1 <= i <= UNITS:
                        exps(i - 1)
                    if i >= LAG:
                        keep_turn(i - LAG)

        @block.vector
        def _(dve):
            def keep(u, kind, c):
                dve.wait_ge(s.product_done, PRODUCTS * u + place[kind, c] + 1)
                bank = mem.banks[other_bank.get((kind, c), 6)]
                if kind == "k":
                    col = BIAS_AT["qkv_b"] + HG + c
                    ins = nc.vector.tensor_scalar(mem.kT[:, c % 2, :], bank[:, :], mem.biasT[:, col:col + 1],
                                                  None, ALU.add)
                elif kind == "q":
                    if u or c:
                        dve.wait_ge(s.queries_alone, UNITS * u + QC * c)
                    ins = nc.vector.tensor_scalar(mem.qT[:, :], bank[:, :], HD ** -0.5,
                                                  mem.q_bias[:, c:c + 1], ALU.mult, ALU.add)
                elif kind == "v":
                    ins = nc.vector.tensor_tensor(mem.v[:, c, :], bank[:, :], mem.bias_tiles[:, 0, :], ALU.add)
                elif kind == "hidden":
                    nc.vector.tensor_tensor(mem.hidden_v[:, :].rearrange("p (h c) -> p h c", h=HG),
                                            bank[:, :].rearrange("p (h c) -> p h c", h=HG),
                                            mem.head_block[:, :].unsqueeze(1).to_broadcast([P, HG, P]),
                                            ALU.mult).then_inc(s.hidden_v, 1)
                    dve.wait_ge(s.hidden_v, u + 1)
                    ins = nc.vector.tensor_tensor(mem.v_extra[:, :, :], mem.v_extra[:, :, :],
                                                  mem.hidden_v[:, :].rearrange("p (h c) -> p h c", h=HG), ALU.add)
                else:
                    ins = nc.vector.tensor_copy(mem.image_scores[:, c % 2, :], bank[:, 0:HPG * QC])
                ins.then_inc(s.product_kept, 1)

            def scores_of(i):
                hg, qc = units[i]
                n = P * (qc + 1)
                slot = i % RING
                if u and i == 0:
                    for q in range(2):
                        dve.wait_ge(s.out_sent[q], 16 * u * QC // 2)
                if i >= RING:
                    dve.wait_ge(s.turned, TURNED * u + turned_by[i - RING + 1])
                for g in range(HPG):
                    dve.wait_ge(s.scores_done, HEADS * u + HPG * i + g + 1)
                    nc.vector.tensor_tensor_reduce(
                        out=mem.probs[:, slot, g, EXTRAS:EXTRAS + n], in0=mem.banks[g][:, 0:n],
                        in1=mem.addends[:, TRI[qc]:TRI[qc] + n], scale=1.0, scalar=LOWEST,
                        op0=ALU.add, op1=ALU.max,
                        accum_out=mem.maxima[:, slot, g:g + 1]).then_inc(s.scores_read, 1)
                dve.wait_ge(s.scores_read, HEADS * u + HPG * (i + 1))
                diag = mem.probs[:, slot, :, EXTRAS + qc * P:EXTRAS + n]
                nc.vector.tensor_tensor(diag, diag, mem.replacing[:, qc, :].unsqueeze(1).to_broadcast([P, HPG, P]), ALU.max)
                dve.wait_ge(s.product_kept, PRODUCTS * u + place["image", hg] + 1)
                image = mem.image_scores[:, hg % 2, HPG * qc:HPG * (qc + 1)]
                nc.vector.tensor_copy(mem.probs[:, slot, :, 1], image)
                nc.vector.scalar_tensor_tensor(out=mem.top[:, :], in0=mem.maxima[:, slot, :],
                                               scalar=mem.masked_max[:, 0:1], in1=image,
                                               op0=ALU.max, op1=ALU.max).then_inc(s.top, 1)
                dve.wait_ge(s.top, UNITS * u + i + 1)
                nc.vector.tensor_scalar(mem.neg_max[:, slot, :], mem.top[:, :], -1.0, None,
                                        ALU.mult).then_inc(s.maxima_ready, 1)

            def normalise(i):
                slot = i % RING
                dve.wait_ge(s.exps_done, HEADS * u + HPG * (i + 1))
                qc = units[i][1]
                nc.vector.scalar_tensor_tensor(out=mem.sums[:, slot, :], in0=mem.probs[:, slot, :, 0],
                                               scalar=mem.tail_sum[:, qc:qc + 1], in1=mem.sums[:, slot, :],
                                               op0=ALU.mult, op1=ALU.add).then_inc(s.scales, 1)
                dve.wait_ge(s.scales, 2 * UNITS * u + 2 * i + 1)
                nc.vector.reciprocal(mem.scales[:, slot, :], mem.sums[:, slot, :]).then_inc(s.scales, 1)
                dve.wait_ge(s.scales, 2 * UNITS * u + 2 * i + 2)
                nc.vector.tensor_tensor(mem.extras[:, slot, :].rearrange("p (g e) -> p g e", e=EXTRAS),
                                        mem.probs[:, slot, :, 0:EXTRAS],
                                        mem.scales[:, slot, :].unsqueeze(2).to_broadcast([P, HPG, EXTRAS]), ALU.mult)
                for g in range(HPG):
                    row = mem.probs[:, slot, g, EXTRAS:EXTRAS + P * (qc + 1)]
                    nc.vector.tensor_scalar(row, row, mem.scales[:, slot, g:g + 1], None,
                                            ALU.mult).then_inc(s.probs_ready, 1)

            for job in early:
                keep(0, *job)
            for u in range(BATCHES):
                dve.wait_ge(s.rows_made, u + 1)
                nc.vector.tensor_scalar(mem.masked_all[:, :], mem.banks[7][:, :], MASK_OUT, None,
                                        ALU.add).then_inc(s.mask_made, 1)
                nc.vector.tensor_copy(mem.mask_all[:, :], mem.banks[7][:, :]).then_inc(s.mask_made, 1)
                nc.vector.tensor_scalar(mem.masked_col[:, :], mem.banks[4][:, 0:QC], MASK_OUT, None, ALU.add)
                dve.wait_ge(s.mask_made, 3 * u + 2)
                nc.vector.tensor_reduce(mem.masked_max[:, :], mem.masked_all[:, :], AX.X, ALU.max).then_inc(s.mask_made, 1)
                dve.wait_ge(s.mask_made, 3 * u + 3)
                nc.vector.tensor_scalar(mem.neg_masked[:, :], mem.masked_max[:, :], -1.0, None,
                                        ALU.mult).then_inc(s.masked_ready, 1)
                for qc in range(QC):
                    at, n = TRI[qc], P * qc
                    if qc:
                        nc.vector.tensor_copy(mem.addends[:, at:at + n], mem.mask_all[:, 0:n])
                    nc.vector.tensor_tensor(mem.addends[:, at + n:at + n + P], mem.mask_all[:, n:n + P],
                                            mem.drop_masked[:, :], ALU.add)
                    ins = nc.vector.tensor_tensor(mem.replacing[:, qc, :], mem.masked_all[:, n:n + P],
                                                  mem.drop_kept[:, :], ALU.add)
                ins.then_inc(s.addends_ready, 1)
                dve.wait_ge(s.addends_ready, u + 1)
                keep(u, "v", 0)
                dve.wait_ge(s.image_made, u + 1)
                nc.vector.tensor_copy(mem.v_extra[:, :, :], mem.banks[5][:, :].rearrange("p (h c) -> p h c", h=HG)).then_inc(s.image_kept, 1)
                for job in at_start[1:]:
                    keep(u, *job)
                dve.wait_ge(s.hidden_exp, u + 1)
                dve.wait_ge(s.image_b, 2 * u + 2)
                for kc in range(1, QC):
                    dst = mem.hidden_w[:, kc - 1, :].rearrange("p (q g e) -> p q g e", q=QC, e=EXTRAS)[:, 0:kc, 0:HPG, 0]
                    nc.vector.tensor_copy(dst, mem.hidden_col[:, kc:kc + 1].unsqueeze(2).to_broadcast([P, kc, HPG]))
                dve.wait_ge(s.image_kept, u + 1)
                for i in range(UNITS + LAG + 2):
                    if i < UNITS:
                        scores_of(i)
                    if 1 <= i <= UNITS:
                        normalise(i - 1)
                    if i < UNITS:
                        for job in at_step[i]:
                            keep(u, *job)
                    elif u + 1 < BATCHES and i < UNITS + len(early):
                        keep(u + 1, *early[i - UNITS])
                    hg = group_ended(i - 1) if i else None
                    if hg is not None:
                        dve.wait_ge(s.weighed, HG * u + hg + 1)
                        nc.vector.tensor_copy(mem.attnT[:, hg, :], mem.banks[7][:, :]).then_inc(s.weighed_kept, 1)
                for tc in range(QC):
                    dve.wait_ge(s.projected, QC * u + tc + 1)
                    if u or tc >= 2:
                        dve.wait_ge(s.out_sent[tc % 2], 16 * (u * QC // 2 + tc // 2))
                    nc.vector.tensor_tensor(mem.out_rows[:, tc % 2, :], mem.banks[tc][:, :],
                                            mem.bias_tiles[:, 1, :], ALU.add).then_inc(s.out_rows, 1)

        @block.gpsimd
        def _(pool):
            def queries_alone(i):
                hg, qc = units[i]
                pool.wait_ge(s.product_kept, PRODUCTS * u + place["q", hg] + 1)
                if i >= 2:
                    pool.wait_ge(s.scores_done, HEADS * u + HPG * (i - 1))
                nc.gpsimd.tensor_tensor(mem.q_alone[:, i % 2, :, :],
                                        mem.qT[:, qc * P:(qc + 1) * P].unsqueeze(1).to_broadcast([P, HPG, P]),
                                        mem.head_rows[:, :].unsqueeze(2).to_broadcast([P, HPG, P]),
                                        ALU.mult).then_inc(s.queries_alone, 1)

            for u in range(BATCHES):
                if u:
                    pool.wait_ge(s.product_done, PRODUCTS * u)
                nc.gpsimd.tensor_copy(mem.k_image_b[:, :, :], mem.k_image[:, batch(u), :, :].rearrange("p o h g -> p (o h) g")).then_inc(s.image_b, 1)
                if u:
                    pool.wait_ge(s.projecting, 2 * u)
                nc.gpsimd.memset(mem.widened[:, :, :], 0.0).then_inc(s.wide_zero, 1)
                pool.wait_ge(s.wide_zero, u + 1)
                nc.gpsimd.tensor_copy(
                    mem.v_image_wide[:, :, :].rearrange("p h (q g e) -> p h q g e", q=QC, e=EXTRAS)[:, :, :, 0:HPG, 1],
                    mem.v_image[:, batch(u), :, :].rearrange("p o h g -> p (o h) g").unsqueeze(2).to_broadcast([P, HG, QC, HPG])).then_inc(s.image_b, 1)
                for i in range(UNITS):
                    queries_alone(i)


class Signals:

    def __init__(self, sem):
        self.all = []

        def new(name):
            self.all.append(sem(name))
            return self.all[-1]

        self.small_in = new("small_in")
        self.weights_in = new("weights_in")
        self.small_turned = new("small_turned")
        self.small_kept = new("small_kept")
        self.bias_kept = new("bias_kept")
        self.zeroed = new("zeroed")
        self.ident = new("ident")
        self.x_turned = new("x_turned")
        self.x_kept0 = new("x_kept0")
        self.x_kept1 = new("x_kept1")
        self.h0_new = new("h0_new")
        self.h12_new = new("h12_new")
        self.main0_done = new("main0_done")
        self.main12_done = new("main12_done")
        self.rows0_copied = new("rows0_copied")
        self.rows12_copied = new("rows12_copied")
        self.turned0 = new("turned0")
        self.turned12 = new("turned12")
        self.pre0 = new("pre0")
        self.pre12 = new("pre12")
        self.gates0 = new("gates0")
        self.gated0 = new("gated0")
        self.memory0 = new("memory0")
        self.tanh0 = new("tanh0")
        self.blend0 = new("blend0")
        self.fresh0 = new("fresh0")
        self.fill_done = new("fill_done")
        self.fill_kept = new("fill_kept")
        self.chunk_op = new("chunk_op")
        self.rows_made = new("rows_made")
        self.turned = new("turned")
        self.turn_kept = new("turn_kept")
        self.image_made = new("image_made")
        self.image_zero = new("image_zero")
        self.image_b = new("image_b")
        self.image_kept = new("image_kept")
        self.queries_alone = new("queries_alone")
        self.head_zero = new("head_zero")
        self.x_in_place = new("x_in_place")
        self.mask_made = new("mask_made")
        self.addends_ready = new("addends_ready")
        self.product_done = new("product_done")
        self.product_kept = new("product_kept")
        self.scores_done = new("scores_done")
        self.scores_read = new("scores_read")
        self.top = new("top")
        self.projecting = new("projecting")
        self.head_wide = new("head_wide")
        self.head_turned = new("head_turned")
        self.hidden_v = new("hidden_v")
        self.masked_ready = new("masked_ready")
        self.hidden_exp = new("hidden_exp")
        self.wide_zero = new("wide_zero")
        self.maxima_ready = new("maxima_ready")
        self.exps_done = new("exps_done")
        self.scales = new("scales")
        self.probs_ready = new("probs_ready")
        self.weighed = new("weighed")
        self.weighed_kept = new("weighed_kept")
        self.projected = new("projected")
        self.out_rows = new("out_rows")
        self.x_in = [new(f"x_in{q}") for q in range(4)]
        self.out_sent = [new(f"out_sent{q}") for q in range(2)]


def build(nc, a, out):
    mem = Mem()
    with ExitStack() as ctx:
        def sb(stack, name, shape):
            return stack.enter_context(nc.sbuf_tensor(name, shape, F32))

        def bank(name):
            return ctx.enter_context(nc.psum_tensor(name, [P, 512], F32))

        sems = Signals(lambda name: ctx.enter_context(nc.semaphore(name)))
        nums = [x.num for x in sems.all]
        assert nums == list(range(nums[0], nums[0] + len(nums)))
        mem.sem_range = range(nums[0], nums[-1] + 1)

        banks = [bank(f"bank{q}") for q in range(8)]
        mem.ps0, mem.ps12, mem.tp0, mem.tp12 = banks[0:4]
        mem.fillps = banks[4:6]
        mem.xps = banks[6:8]

        mem.X = sb(ctx, "X", [P, KC, B, T])
        mem.ident = sb(ctx, "ident", [P, P])
        mem.biasT = sb(ctx, "biasT", [P, NBIAS])
        mem.condT = sb(ctx, "condT", [P, KC, B])
        mem.banks = banks

        mem.w_qkv = sb(ctx, "w_qkv", [P, KC, 3 * D])
        mem.wh0 = sb(ctx, "wh0", [P, KC, KC, G0 // KC * P])
        parts = mem.wh0[:, :, :, :].rearrange("p k j c -> p (k j c)").rearrange("p (s k n) -> p s k n", s=3, k=KC)
        mem.w_proj, mem.xT, mem.attnT = (parts[:, q, :, :] for q in range(3))
        mem.uk_rows, mem.uv_rows = mem.xT, mem.attnT

        with ExitStack() as scan:
            mem.h0 = sb(scan, "h0", [P, SLOTS, KC, CH, B])
            mem.h12 = sb(scan, "h12", [P, SLOTS, 2, KC, CH, B])
            mem.wx = [mem.w_qkv, sb(scan, "wx1", [P, KC, D]), sb(scan, "wx2", [P, KC, D])]
            mem.wh12 = sb(scan, "wh12", [P, 2, KC, D])
            mem.xw0 = sb(scan, "xw0", [P, SLOTS, XW, CH, B])
            mem.xw12 = sb(scan, "xw12", [P, SLOTS, 2, KC, CH, B])
            mem.stage = [sb(scan, f"stage{l}", [P, KC, N]) for l in range(3)]
            mem.rows0 = sb(scan, "rows0", [P, G0 // KC * P])
            mem.rows12 = sb(scan, "rows12", [P, 2 * P])
            mem.pre0 = sb(scan, "pre0_sb", [P, G0, B])
            mem.gates0 = sb(scan, "gates0_sb", [P, 2 * KC, B])
            mem.gated0 = sb(scan, "gated0_sb", [P, KC, B])
            mem.mem0 = sb(scan, "mem0", [P, KC, B])
            mem.tanh0 = sb(scan, "tanh0_sb", [P, KC, B])
            mem.keep0 = sb(scan, "keep0", [P, KC, B])
            mem.held0 = sb(scan, "held0", [P, KC, B])
            mem.fresh0 = sb(scan, "fresh0_sb", [P, KC, B])
            mem.sum12 = sb(scan, "sum12", [P, 2, 4, B])
            with ExitStack() as load:
                mem.xrows = sb(load, "xrows", [P, 4, D])
                mem.bias_rows = sb(load, "bias_rows", [P, P])
                mem.cond_rows = sb(load, "cond_rows", [P, D])
                setup(nc, mem, sems, a)
                clear_signals(nc, mem)
            m = 0
            while m < ROUNDS:
                times = (NCH - 1 - m) // PER_BLOCK if m == RAMP else 1
                scan_rounds(nc, mem, sems, a, m, times)
                m += PER_BLOCK * times
            add_last_chunk(nc, mem)
            clear_signals(nc, mem)

        mem.bias_tiles = sb(ctx, "bias_tiles", [P, 2, D])
        mem.drop_masked = sb(ctx, "drop_masked", [P, P])
        mem.drop_kept = sb(ctx, "drop_kept", [P, P])
        mem.ones = sb(ctx, "ones", [P, P])
        mem.k_image = sb(ctx, "k_image", [P, B, HG, HPG])
        mem.v_image = sb(ctx, "v_image", [P, B, HG, HPG])
        mem.head_rows = sb(ctx, "head_rows", [P, HPG])
        mem.q_bias = sb(ctx, "q_bias", [P, HG])
        mem.probsT = sb(ctx, "probsT", [P, HPG, QC, T])
        mem.row_biases = mem.probsT[:, 0, 0:2, :]
        mem.probs_extra = sb(ctx, "probs_extra", [P, T])
        mem.head_block = sb(ctx, "head_block", [P, P])
        mem.tail_sum = sb(ctx, "tail_sum", [P, QC])
        mem.head_wide = mem.probsT[:, 1, 0, 0:P]
        mem.q_alone = sb(ctx, "q_alone", [P, 2, HPG, P])
        attention_setup(nc, mem, sems, a)
        clear_signals(nc, mem)
        mem.qT = sb(ctx, "qT", [P, T])
        mem.kT = sb(ctx, "kT", [P, 2, T])
        mem.v = sb(ctx, "v", [P, QC, D])
        mem.probs = sb(ctx, "probs", [P, RING, HPG, EXTRAS + T])
        mem.extras = sb(ctx, "extras", [P, RING, HPG * EXTRAS])
        mem.mask_row = sb(ctx, "mask_row", [P, T])
        mem.mask_all = mem.v[:, 0, :]
        mem.widened = mem.attnT[:, 0:2, :]
        mem.v_image_wide = mem.attnT[:, 0, :].rearrange("p (h c) -> p h c", h=HG)
        mem.hidden_w = mem.attnT[:, 1, 0:(QC - 1) * P].rearrange("p (k c) -> p k c", k=QC - 1)
        mem.hidden_rows = mem.probs[:, RING - 1, :, :]
        mem.masked_all = mem.attnT[:, 3, :]
        mem.hidden_v = mem.attnT[:, 3, :]
        mem.masked_col = sb(ctx, "masked_col", [P, QC])
        mem.hidden_col = sb(ctx, "hidden_col", [P, QC])
        mem.neg_masked = sb(ctx, "neg_masked", [P, 1])
        mem.masked_max = sb(ctx, "masked_max", [P, 1])
        mem.addends = sb(ctx, "addends", [P, TRI[-1]])
        mem.replacing = sb(ctx, "replacing", [P, QC, P])
        mem.image_scores = sb(ctx, "image_scores", [P, 2, HPG * QC])
        mem.k_image_b = sb(ctx, "k_image_b", [P, HG, HPG])
        mem.v_extra = sb(ctx, "v_extra", [P, HG, P])
        mem.maxima = sb(ctx, "maxima", [P, RING, HPG])
        mem.top = sb(ctx, "top_sb", [P, HPG])
        mem.neg_max = sb(ctx, "neg_max", [P, RING, HPG])
        mem.sums = sb(ctx, "sums", [P, RING, HPG])
        mem.scales = sb(ctx, "scales_sb", [P, RING, HPG])
        mem.out_rows = mem.probs[:, 0:1, 0:2, 0:T].rearrange("p r g t -> p (r g) t")
        with nc.Fori(0, B // BATCHES) as part:
            attention_batches(nc, mem, sems, a, out, part)
            clear_signals(nc, mem)


_INPUTS = {"x": "x", "cond": "cond_1024", "mask": "mask_Bx1x1xS_ff0",
           "w_W": "L0_cond_w_W", "w_b": "L0_cond_w_b", "wx_W": "L0_cond_wx_W", "wx_b": "L0_cond_wx_b",
           "wh_W": "L0_cond_wh_W", "wh_b": "L0_cond_wh_b", "L1_Wx": "L1_cond_Wx", "L1_Wh": "L1_cond_Wh",
           "L1_b": "L1_cond_b", "L2_Wx": "L2_cond_Wx", "L2_Wh": "L2_cond_Wh", "L2_b": "L2_cond_b",
           "qkv_w": "L3_cond_c_attn_w", "qkv_b": "L3_cond_c_attn_b", "proj_w": "L3_cond_c_proj_w",
           "proj_b": "L3_cond_c_proj_b", "uk_w": "L3_cond_uk_w", "uk_b": "L3_cond_uk_b",
           "uv_w": "L3_cond_uv_w", "uv_b": "L3_cond_uv_b"}


def kernel(**inputs):
    import numpy as _np
    import concourse.bacc as _bacc
    from concourse import mybir as _mybir
    from concourse.bass_utils import run_bass_kernel_spmd as _run

    nc = _bacc.Bacc("TRN2", target_bir_lowering=False, num_devices=1)
    arrays, args = {}, {}
    for short, name in _INPUTS.items():
        v = _np.ascontiguousarray(inputs[name])
        arrays[f"in_{name}_dram"] = v
        args[short] = nc.dram_tensor(f"in_{name}_dram", v.shape, _mybir.dt.from_np(v.dtype), kind="ExternalInput").ap()
    args["mask"] = args["mask"].rearrange("b o1 o2 t -> (b o1 o2) t")
    out = nc.dram_tensor("out_0_dram", (8, 512, 512), _mybir.dt.float32, kind="ExternalOutput").ap()
    build(nc, args, out)
    r = _run(nc, [arrays], core_ids=[0])
    return r.results[0]["out_0_dram"]
```
